# Optimizing a Trainium2 kernel written in Bass

```python
import numpy as np
import jax
import jax.numpy as jnp

def _softmax(x, axis=-1):
    return jax.nn.softmax(x, axis=axis)

def _gelu(x):
    return jax.nn.gelu(x, approximate=True)

def _silu(x):
    return jax.nn.silu(x)

def _sigmoid(x):
    return jax.nn.sigmoid(x)

def _layernorm(x, axis=-1, eps=1e-05):
    m = jnp.mean(x, axis=axis, keepdims=True)
    v = jnp.var(x, axis=axis, keepdims=True)
    return (x - m) / jnp.sqrt(v + eps)

def _scatter_add(tgt, idx, src, axis=0):
    return tgt.at[idx].add(src)

def _segment_sum(src, seg, n):
    return jax.ops.segment_sum(src, seg, n)
kernel_name = 'mk_cond_resid_d2_seqx_r8_6b4e1d'

def setup_inputs(seed: int=0):
    np.random.seed(seed)
    _w = jnp.asarray

    def _rec_inputs():
        import jax
        import jax.numpy as jnp
        _rk = jax.random.key(seed)
        x = -0.0001538 + 1 * jax.random.normal(jax.random.fold_in(_rk, 1), (8, 128, 128), jnp.float32)
        _lenS = 128 - jax.random.randint(jax.random.fold_in(_rk, 7), (8,), 0, max(1, 128 // 4) + 1, jnp.int32)
        _lenS2 = 128 - jax.random.randint(jax.random.fold_in(_rk, 8), (8,), 0, max(1, 128 // 4) + 1, jnp.int32)
        cond_1024 = 0.00782532 + 1.00527 * jax.random.normal(jax.random.fold_in(_rk, 11), (8, 128), jnp.float32)
        return (x, cond_1024)
    x, cond_1024 = _rec_inputs()

    def _L0_cond_setup():
        import jax, jax.numpy as jnp
        import numpy as np
        NUM_EXPERTS = 4
        TOP_K = 2
        key = jax.random.key(seed)
        ks = jax.random.split(key, 16)
        B, L, D, E, H = (8, 96, 128, NUM_EXPERTS, 512)
        s = 0.02
        return {'context_c': jax.random.normal(ks[0], (B, L, D), jnp.float32), 'time_cond': jax.random.normal(ks[1], (B, D), jnp.float32), 'gate_w': jax.random.normal(ks[2], (3 * D, E), jnp.float32) * s, 'gate_b': jnp.zeros((E,), jnp.float32), 'time_w': jax.random.normal(ks[3], (D, 2 * E), jnp.float32) * s, 'time_b': jnp.zeros((2 * E,), jnp.float32), 'ew1': jax.random.normal(ks[4], (E, D, H), jnp.float32) * s, 'eb1': jnp.zeros((E, H), jnp.float32), 'ew2': jax.random.normal(ks[5], (E, H, D), jnp.float32) * s, 'eb2': jnp.zeros((E, D), jnp.float32), 'sw1': jax.random.normal(ks[6], (D, H), jnp.float32) * s, 'sb1': jnp.zeros((H,), jnp.float32), 'sw2': jax.random.normal(ks[7], (H, D), jnp.float32) * s, 'sb2': jnp.zeros((D,), jnp.float32)}
    _L0_cond_all = _L0_cond_setup()
    _L0_cond_in = {k: v for k, v in _L0_cond_all.items() if k in ('gate_w', 'gate_b', 'time_w', 'time_b', 'ew1', 'eb1', 'ew2', 'eb2', 'sw1', 'sb1', 'sw2', 'sb2')}
    del _L0_cond_all

    def _L1_cond_setup():
        import jax, jax.numpy as jnp
        import numpy as np
        RANK = 8
        LN_EPS = 1e-05
        key = jax.random.key(seed)
        ks = jax.random.split(key, 8)
        B, T, D = (16, 128, 128)
        A = 128
        I = 128
        OUT = D * RANK * 4
        s = 0.02
        return {'x': jax.random.normal(ks[0], (B, T, D), jnp.float32), 'ada_emb': jax.random.normal(ks[1], (B, A), jnp.float32), 'base_up': jax.random.normal(ks[2], (D, D), jnp.float32) * s, 'base_down': jax.random.normal(ks[3], (D, D), jnp.float32) * s, 'ln_gamma': jnp.ones((A,), jnp.float32), 'ln_beta': jnp.zeros((A,), jnp.float32), 'W1': jax.random.normal(ks[4], (A, I), jnp.float32) / np.sqrt(A), 'bias1': jnp.zeros((I,), jnp.float32), 'W2': jax.random.normal(ks[5], (I, OUT), jnp.float32) / np.sqrt(I), 'bias2': jnp.zeros((OUT,), jnp.float32)}
    _L1_cond_all = _L1_cond_setup()
    _L1_cond_in = {k: v for k, v in _L1_cond_all.items() if k in ('base_up', 'base_down', 'ln_gamma', 'ln_beta', 'W1', 'bias1', 'W2', 'bias2')}
    del _L1_cond_all
    return {'x': x, 'cond_1024': cond_1024, 'L0_cond_gate_w': _L0_cond_in['gate_w'], 'L0_cond_gate_b': _L0_cond_in['gate_b'], 'L0_cond_time_w': _L0_cond_in['time_w'], 'L0_cond_time_b': _L0_cond_in['time_b'], 'L0_cond_ew1': _L0_cond_in['ew1'], 'L0_cond_eb1': _L0_cond_in['eb1'], 'L0_cond_ew2': _L0_cond_in['ew2'], 'L0_cond_eb2': _L0_cond_in['eb2'], 'L0_cond_sw1': _L0_cond_in['sw1'], 'L0_cond_sb1': _L0_cond_in['sb1'], 'L0_cond_sw2': _L0_cond_in['sw2'], 'L0_cond_sb2': _L0_cond_in['sb2'], 'L1_cond_base_up': _L1_cond_in['base_up'], 'L1_cond_base_down': _L1_cond_in['base_down'], 'L1_cond_ln_gamma': _L1_cond_in['ln_gamma'], 'L1_cond_ln_beta': _L1_cond_in['ln_beta'], 'L1_cond_W1': _L1_cond_in['W1'], 'L1_cond_bias1': _L1_cond_in['bias1'], 'L1_cond_W2': _L1_cond_in['W2'], 'L1_cond_bias2': _L1_cond_in['bias2']}

def reference(x, cond_1024, L0_cond_gate_w, L0_cond_gate_b, L0_cond_time_w, L0_cond_time_b, L0_cond_ew1, L0_cond_eb1, L0_cond_ew2, L0_cond_eb2, L0_cond_sw1, L0_cond_sb1, L0_cond_sw2, L0_cond_sb2, L1_cond_base_up, L1_cond_base_down, L1_cond_ln_gamma, L1_cond_ln_beta, L1_cond_W1, L1_cond_bias1, L1_cond_W2, L1_cond_bias2):
    import jax
    import jax.numpy as jnp

    def _L0_cond_ref(context_c, time_cond, gate_w, gate_b, time_w, time_b, ew1, eb1, ew2, eb2, sw1, sb1, sw2, sb2):
        import jax, jax.numpy as jnp
        import numpy as np
        NUM_EXPERTS = 4
        TOP_K = 2
        B, L, D = context_c.shape
        E, K = (NUM_EXPERTS, TOP_K)
        L_head = L_wrist = L // 3
        head = context_c[:, :L_head]
        wrist = context_c[:, L_head:L_head + L_wrist]
        proprio = context_c[:, L_head + L_wrist:]
        full_agg = context_c.mean(axis=1)
        hp_agg = jnp.concatenate([head, proprio], axis=1).mean(axis=1)
        wp_agg = jnp.concatenate([wrist, proprio], axis=1).mean(axis=1)
        gate_in = jnp.concatenate([full_agg, hp_agg, wp_agg], axis=-1)
        gate_logits = gate_in @ gate_w + gate_b
        mod = jax.nn.silu(time_cond) @ time_w + time_b
        scale, shift = jnp.split(mod, 2, axis=-1)
        gate_logits = gate_logits * (1.0 + scale) + shift
        gate_scores = jax.nn.softmax(gate_logits, axis=-1)
        topk_w, topk_i = jax.lax.top_k(gate_scores, K)
        topk_w = topk_w / (topk_w.sum(axis=-1, keepdims=True) + 1e-08)
        onehot = (topk_i[..., None] == jnp.arange(E)[None, None, :]).astype(context_c.dtype)
        w_be = jnp.sum(topk_w[..., None] * onehot, axis=1)
        mask = np.ones((E, L), dtype=np.float32)
        mask[1, L_head:L_head + L_wrist] = 0.0
        mask[2, :L_head] = 0.0
        mask = jnp.asarray(mask)
        out = jnp.zeros_like(context_c)
        for e in range(E):
            h = jax.nn.gelu(context_c @ ew1[e] + eb1[e], approximate=True)
            y = h @ ew2[e] + eb2[e]
            out = out + w_be[:, e][:, None, None] * mask[e][None, :, None] * y
        shared = jax.nn.gelu(context_c @ sw1 + sb1, approximate=True) @ sw2 + sb2
        return out + shared

    def _L1_cond_ref(x, ada_emb, base_up, base_down, ln_gamma, ln_beta, W1, bias1, W2, bias2):
        import jax, jax.numpy as jnp
        import numpy as np
        RANK = 8
        LN_EPS = 1e-05
        B, T, D = x.shape
        R = RANK
        mu = jnp.mean(ada_emb, axis=-1, keepdims=True)
        var = jnp.mean(jnp.square(ada_emb - mu), axis=-1, keepdims=True)
        c = (ada_emb - mu) / jnp.sqrt(var + LN_EPS) * ln_gamma + ln_beta
        h = jax.nn.gelu(c @ W1 + bias1, approximate=False)
        w = h @ W2 + bias2
        a1, b1, a2, b2 = [t.reshape(B, D, R) for t in jnp.split(w, 4, axis=-1)]
        u = jnp.einsum('btd,bdr->btr', x, a2)
        mid = jnp.einsum('btd,dl->btl', x, base_down) + jnp.einsum('btr,blr->btl', u, b2)
        mid = jax.nn.gelu(mid, approximate=False)
        v = jnp.einsum('blr,btl->btr', b1, mid)
        out = jnp.einsum('btl,kl->btk', mid, base_up) + jnp.einsum('bkr,btr->btk', a1, v)
        return x + out
    x = x + _L0_cond_ref(x, cond_1024, L0_cond_gate_w, L0_cond_gate_b, L0_cond_time_w, L0_cond_time_b, L0_cond_ew1, L0_cond_eb1, L0_cond_ew2, L0_cond_eb2, L0_cond_sw1, L0_cond_sb1, L0_cond_sw2, L0_cond_sb2)
    x = x + _L1_cond_ref(x, cond_1024, L1_cond_base_up, L1_cond_base_down, L1_cond_ln_gamma, L1_cond_ln_beta, L1_cond_W1, L1_cond_bias1, L1_cond_W2, L1_cond_bias2)
    return x

_drawn_inputs = setup_inputs


def setup_inputs(seed=0):
    import zlib

    import numpy as np

    out = dict(_drawn_inputs(seed))
    spreads = {'L0_cond_gate_b': (0.0, 0.29),
     'L0_cond_time_b': (0.0, 0.1),
     'L0_cond_eb1': (0.0, 0.453),
     'L0_cond_eb2': (0.0, 0.1),
     'L0_cond_sb1': (0.0, 0.31),
     'L0_cond_sb2': (0.0, 0.1),
     'L1_cond_ln_gamma': (1.0, 0.2),
     'L1_cond_ln_beta': (0.0, 0.1),
     'L1_cond_bias1': (0.0, 0.1),
     'L1_cond_bias2': (0.0, 0.1)}
    factors = {'L1_cond_base_up': 3.923, 'L1_cond_base_down': 3.745, 'L0_cond_gate_w': 3.507}
    for name, (base, spread) in spreads.items():
        noise = np.random.default_rng([zlib.crc32(name.encode()), seed]).standard_normal(out[name].shape)
        drawn = base * np.exp(spread * noise) if base else spread * noise
        out[name] = jnp.asarray(drawn.astype(out[name].dtype))
    for name, factor in factors.items():
        out[name] = (out[name] * factor).astype(out[name].dtype)
    return out
```

```python
from contextlib import ExitStack

import concourse.bass as bass
from concourse import mybir

ALU = mybir.AluOpType
ACT = mybir.ActivationFunctionType
AX = mybir.AxisListType
F32 = mybir.dt.float32
F32R = mybir.dt.float32r


def moe_lowrank_kernel(nc, x, cond, gate_w, gate_b, time_w, time_b, ew1, eb1, ew2, eb2, sw1, sb1, sw2, sb2,
                       base_up, base_down, ln_gamma, ln_beta, W1, bias1, W2, bias2, out):
    B, T, D = x.shape
    E, _, H = ew1.shape
    NE = E + 1
    SHARED = E
    NC = H // 128
    Q = 4
    R = W2.shape[1] // (Q * D)
    L3 = T // 3
    HEAD, PROP = L3, T - 2 * L3
    REGIONS = ((0, 0, HEAD), (2 * L3, HEAD, PROP), (L3, HEAD + PROP, L3))
    SPAN = {0: (0, T), 1: (0, HEAD + PROP), 2: (HEAD, T), 3: (0, T), SHARED: (0, T)}
    HALVES = 2
    HB = B // HALVES
    ORDER = (SHARED, 0, 1, 2, 3)
    CHUNKS = HALVES * NE * NC
    LAG = 2
    NZ, NH = 3, 4
    EPS = 1e-5

    def unit(i):
        u = i // NC
        return u // NE, ORDER[u % NE], i % NC, u

    with ExitStack() as ctx:
        def sb(name, shape, dt=F32):
            return ctx.enter_context(nc.sbuf_tensor(name, shape, dt))

        def pb(name):
            return ctx.enter_context(nc.psum_tensor(name, [128, 512], F32))

        def sem(name):
            return ctx.enter_context(nc.semaphore(name))

        ident = sb("ident", [128, 128])
        two_i = sb("two_i", [128, 128])
        means = sb("means", [128, 3])
        ones = sb("ones", [8, 128])
        half_neg = sb("half_neg", [8, 1])
        own = sb("own", [64, HB])
        order_mask = sb("order_mask", [8, E, 2, E])
        x_tok = sb("x_tok", [128, B, D])
        rows = sb("rows", [36, 128])
        gw = sb("gw", [128, 3, E])
        tw = sb("tw", [128, 2 * E])
        gtb = sb("gtb", [1, 3 * E])
        w1 = sb("w1", [128, NE, H])
        w2 = sb("w2", [128, NE, NC, D])
        W1_s = sb("W1_s", [128, 128])
        down = sb("down", [128, 128])
        up = sb("up", [128, 128])
        b2c = sb("b2c", [128, Q, R])
        W2_s = sb("W2_s", [128, Q * D * R])
        w1_hi, w1_lo = sb("w1_hi", [128, NE, H], F32R), sb("w1_lo", [128, NE, H], F32R)
        w2_hi, w2_lo = sb("w2_hi", [128, NE, NC, D], F32R), sb("w2_lo", [128, NE, NC, D], F32R)
        x_hi, x_lo = sb("x_hi", [128, B, T], F32R), sb("x_lo", [128, B, T], F32R)
        h = sb("h", [128, NH, 512])
        h_hi, h_lo = sb("h_hi", [128, NH, 512], F32R), sb("h_lo", [128, NH, 512], F32R)
        xT = sb("xT", [128, B, T])
        acc = sb("acc", [128, B, T])
        mid = sb("mid", [128, B, T])
        o_tok = sb("o_tok", [128, B, D])
        cols = sb("cols", [128, 36])
        EB1, EB2, SB2, BIAS1, GAMMA, BETA = 8, 28, 32, 33, 34, 35
        pooled = sb("pooled", [128, B, 3])
        sil = sb("sil", [128, 4, B])
        mod_s = sb("mod_s", [8, 2 * E])
        lg = sb("lg", [8, 8, E])
        sc = sb("sc", [8, 8])
        cmp = sb("cmp", [8, E, 2, E])
        cmpm = sb("cmpm", [8, E, 2, E])
        wdiag = sb("wdiag", [8, B, E])
        wbc = sb("wbc", [128, B, E])
        br = sb("br", [128, 5, B])
        stats = sb("stats", [8, 6])
        mv = sb("mv", [8, 4])
        cn = sb("cn", [8, 128])
        cT = sb("cT", [128, B])
        hc = sb("hc", [128, B])
        lr = sb("lr", [128, Q, B * R])
        lT = sb("lT", [64, 2, 128])
        lM = sb("lM", [64, 2, HB, 128])
        upT = sb("upT", [128, 128])
        WM = sb("WM", [128, B, 128])
        WO = sb("WO", [128, B, 128])

        Z = [pb(f"Z{i}") for i in range(NZ)]
        Y = [pb(f"Y{i}") for i in range(2)]
        S = [pb(f"S{i}") for i in range(3)]

        x_in = [sem(f"x_in{i}") for i in range(HALVES)]
        rows_in = sem("rows_in")
        gate_in = sem("gate_in")
        w1_in = [sem(f"w1_in{e}") for e in range(NE)]
        w2_in = [sem(f"w2_in{e}") for e in range(NE)]
        base_in = sem("base_in")
        W2_in = sem("W2_in")
        out_done = sem("out_done")

        ident0 = sem("ident0")
        ident_ok = sem("ident_ok")
        consts0 = sem("consts0")
        consts1 = sem("consts1")
        consts_ok = sem("consts_ok")
        rstd_ok = sem("rstd_ok")
        pool_lo = sem("pool_lo")

        rowsT_ok = sem("rowsT_ok")
        xT_ok = sem("xT_ok")
        pooled_ok = sem("pooled_ok")
        cnT_ok = sem("cnT_ok")
        logit_ok = sem("logit_ok")
        wbc_ok = sem("wbc_ok")
        hpre_ok = sem("hpre_ok")
        upT_ok = sem("upT_ok")
        adapt_ok = sem("adapt_ok")
        lT_ok = sem("lT_ok")
        merge_ok = sem("merge_ok")
        z_ok = sem("z_ok")
        y_ok = sem("y_ok")
        mid_ok = sem("mid_ok")
        o_ok = sem("o_ok")

        cols_ok = sem("cols_ok")
        exp_sil = sem("exp_sil")
        xT_copied = sem("xT_copied")
        exp_ok = sem("exp_ok")
        hc_ok = sem("hc_ok")
        h_ok = sem("h_ok")
        hi_ok = sem("hi_ok")
        midg_ok = sem("midg_ok")

        ln_step = sem("ln_step")
        cn_ok = sem("cn_ok")
        cT_step = sem("cT_step")
        x_split = sem("x_split")
        w_hi_ok = sem("w_hi_ok")
        w_lo_ok = sem("w_lo_ok")
        pooled_copied = sem("pooled_copied")
        sil_step = sem("sil_step")
        gate_step = sem("gate_step")
        nmax_ok = sem("nmax_ok")
        wdiag_ok = sem("wdiag_ok")
        wbc_copied = sem("wbc_copied")
        br_step = sem("br_step")
        xb_ok = sem("xb_ok")
        upT_copied = sem("upT_copied")
        lr_ok = sem("lr_ok")
        lT_copied = sem("lT_copied")
        merged = sem("merged")
        lo_ok = sem("lo_ok")
        acc_ok = sem("acc_ok")
        acc_part = sem("acc_part")
        o_copied = sem("o_copied")

        DVE_LO = 2

        def w_parts(k):
            e = ORDER[k // 2]
            if k % 2 == 0:
                return w1[:, e], w1_hi[:, e], w1_lo[:, e], w1_in[e]
            return (w2[:, e].rearrange("p c d -> p (c d)"), w2_hi[:, e].rearrange("p c d -> p (c d)"),
                    w2_lo[:, e].rearrange("p c d -> p (c d)"), w2_in[e])

        def wait_split(eng, k):
            if k < DVE_LO:
                eng.wait_ge(w_lo_ok, k + 1)
            else:
                eng.wait_ge(pool_lo, k - DVE_LO + 1)

        block = ctx.enter_context(nc.Block())

        @block.sync
        def _(sp):
            def load_x(hf):
                for t0, p0, n in REGIONS:
                    sp.dma_start(x_tok[p0:p0 + n, hf * HB:(hf + 1) * HB, :],
                                 x[hf * HB:(hf + 1) * HB, t0:t0 + n, :].rearrange("b t d -> t b d")
                                 ).then_inc(x_in[hf], 16)

            def load_w1(e):
                sp.dma_start(w1[:, e, :], sw1 if e == SHARED else ew1[e]).then_inc(w1_in[e], 16)

            def load_w2(e):
                src = sw2 if e == SHARED else ew2[e]
                sp.dma_start(w2[:, e], src.rearrange("(c p) d -> p c d", p=128)).then_inc(w2_in[e], 16)

            load_x(0)
            load_w1(SHARED)
            load_x(1)
            load_w2(SHARED)
            for e in ORDER[1:3]:
                load_w1(e)
                load_w2(e)
            half_w = Q * D * R // 2
            for c in range(2):
                sp.dma_start(W2_s[:, c * half_w:(c + 1) * half_w], W2[:, c * half_w:(c + 1) * half_w]).then_inc(W2_in, 16)
            for e in ORDER[3:]:
                load_w1(e)
                load_w2(e)
            for hf in range(HALVES):
                sp.wait_ge(o_copied, hf + 1)
                for t0, p0, n in REGIONS:
                    sp.dma_start(out[hf * HB:(hf + 1) * HB, t0:t0 + n, :].rearrange("b t d -> t b d"),
                                 o_tok[p0:p0 + n, hf * HB:(hf + 1) * HB, :]).then_inc(out_done, 16)
            sp.wait_ge(out_done, 16 * 3 * HALVES)

        @block.gpsimd
        def _(pool):
            pool.memset(ident[:], 0.0).then_inc(ident0, 1)
            pool.wait_ge(ident0, 1)
            pool.affine_select(out=ident[:], in_=ident[:], compare_op=ALU.not_equal, fill=1.0, base=0,
                               pattern=[[-1, 128]], channel_multiplier=1).then_inc(ident_ok, 1)
            pool.memset(two_i[:], 0.0).then_inc(consts0, 1)
            pool.memset(means[:, 0:1], 1.0 / T).then_inc(consts0, 1)
            pool.memset(means[:, 1:3], 1.0 / (HEAD + PROP)).then_inc(consts0, 1)
            pool.memset(own[:], 1.0).then_inc(consts0, 1)
            pool.memset(order_mask[:], 1.0).then_inc(consts0, 1)
            pool.memset(half_neg[:], -0.5).then_inc(consts_ok, 1)
            pool.memset(ones[:], 1.0).then_inc(consts_ok, 1)
            pool.wait_ge(consts0, 5)
            pool.affine_select(out=means[:, 1:2], in_=means[:, 1:2], compare_op=ALU.is_ge, fill=0.0,
                               base=HEAD + PROP - 1, pattern=[[0, 1]], channel_multiplier=-1).then_inc(consts_ok, 1)
            pool.affine_select(out=means[:, 2:3], in_=means[:, 2:3], compare_op=ALU.is_ge, fill=0.0,
                               base=-HEAD, pattern=[[0, 1]], channel_multiplier=1).then_inc(consts_ok, 1)
            pool.affine_select(out=order_mask[:, :, 0, :], in_=order_mask[:, :, 0, :], compare_op=ALU.is_gt, fill=0.0,
                               base=0, pattern=[[1, E], [-1, E]], channel_multiplier=0).then_inc(consts_ok, 1)
            pool.affine_select(out=order_mask[:, :, 1, :], in_=order_mask[:, :, 1, :], compare_op=ALU.is_gt, fill=0.0,
                               base=0, pattern=[[-1, E], [1, E]], channel_multiplier=0).then_inc(consts_ok, 1)
            pool.affine_select(out=two_i[:], in_=two_i[:], compare_op=ALU.not_equal, fill=2.0, base=0,
                               pattern=[[-1, 128]], channel_multiplier=1).then_inc(consts_ok, 1)
            for hf in range(HALVES):
                o = own[hf * HB * R:(hf + 1) * HB * R, :]
                pool.affine_select(out=o, in_=o, compare_op=ALU.is_ge, fill=0.0, base=0,
                                   pattern=[[-R, HB]], channel_multiplier=1).then_inc(consts1, 1)
                pool.wait_ge(consts1, hf + 1)
                pool.affine_select(out=o, in_=o, compare_op=ALU.is_ge, fill=0.0, base=R - 1,
                                   pattern=[[R, HB]], channel_multiplier=-1).then_inc(consts_ok, 1)
            pool.wait_ge(ln_step, 3)
            pool.tensor_tensor(mv[:, 3:4], mv[:, 2:3], half_neg[:], ALU.pow).then_inc(rstd_ok, 1)
            for k in range(DVE_LO, 2 * NE):
                raw, hi, lo, _ = w_parts(k)
                pool.wait_ge(w_hi_ok, k + 1)
                pool.tensor_tensor(lo, raw, hi.bitcast(F32), ALU.subtract).then_inc(pool_lo, 1)

        N_CONSTS = 9

        @block.scalar
        def _(act):
            act.dma_start(rows[0:8, :], cond).then_inc(rows_in, 16)
            act.dma_start(rows[8:24, :], eb1.rearrange("e (c p) -> (e c) p", p=128)).then_inc(rows_in, 16)
            act.dma_start(rows[24:28, :], sb1.rearrange("(c p) -> c p", p=128)).then_inc(rows_in, 16)
            act.dma_start(rows[28:32, :], eb2).then_inc(rows_in, 16)
            for n, v in ((32, sb2), (33, bias1), (34, ln_gamma), (35, ln_beta)):
                act.dma_start(rows[n:n + 1, :], v.rearrange("(a n) -> a n", a=1)).then_inc(rows_in, 16)
            act.dma_start(gw[:], gate_w.rearrange("(k p) e -> p k e", p=128)).then_inc(gate_in, 16)
            act.dma_start(tw[:], time_w).then_inc(gate_in, 16)
            act.dma_start(gtb[:, 0:E], gate_b.rearrange("(a n) -> a n", a=1)).then_inc(gate_in, 16)
            act.dma_start(gtb[:, E:3 * E], time_b.rearrange("(a n) -> a n", a=1)).then_inc(gate_in, 16)
            act.dma_start(W1_s[:], W1).then_inc(base_in, 16)
            act.dma_start(down[:], base_down).then_inc(base_in, 16)
            act.dma_start(up[:], base_up).then_inc(base_in, 16)
            act.dma_start(b2c[:], bias2.rearrange("(q d r) -> d q r", q=Q, r=R)).then_inc(base_in, 16)

            act.wait_ge(rowsT_ok, 1)
            nc.scalar.activation(cols[:], S[0][:, 0:36], ACT.Copy).then_inc(cols_ok, 1)
            act.wait_ge(cols_ok, 1)
            nc.scalar.activation(sil[:, 0, :], cols[:, 0:8], ACT.Exp, scale=-1.0).then_inc(exp_sil, 1)
            for hf in range(HALVES):
                act.wait_ge(xT_ok, hf + 1)
                nc.scalar.activation(xT[:, hf * HB:(hf + 1) * HB, :].rearrange("p b t -> p (b t)"), Y[hf][:],
                                     ACT.Copy).then_inc(xT_copied, 1)
            act.wait_ge(nmax_ok, 1)
            nc.scalar.activation(lg[:, 2, :], lg[:, 1, :], ACT.Exp, bias=sc[:, 0:1],
                                 accum_out=sc[:, 1:2]).then_inc(exp_ok, 1)
            act.wait_ge(hpre_ok, 1)
            nc.scalar.activation(hc[:], S[2][:, 16:24], ACT.Gelu, bias=cols[:, BIAS1:BIAS1 + 1]).then_inc(hc_ok, 1)

            def gelu(i):
                _, e, c, _ = unit(i)
                lo, hi = SPAN[e]
                n = HB * (hi - lo)
                act.wait_ge(z_ok, i + 1)
                if i >= NH:
                    act.wait_ge(lo_ok, i - NH + 1)
                b = EB1 + e * NC + c
                nc.scalar.activation(h[:, i % NH, 0:n], Z[i % NZ][:, 0:n], ACT.Gelu_apprx_tanh,
                                     bias=cols[:, b:b + 1]).then_inc(h_ok, 1)

            def hidden_hi(i):
                _, e, _, _ = unit(i)
                lo, hi = SPAN[e]
                n = HB * (hi - lo)
                act.wait_ge(h_ok, i + 1)
                if i >= NH:
                    act.wait_ge(y_ok, i - NH + 1)
                nc.scalar.activation(h_hi[:, i % NH, 0:n], h[:, i % NH, 0:n], ACT.Copy).then_inc(hi_ok, 1)

            for i in range(CHUNKS + 1):
                if i < CHUNKS:
                    gelu(i)
                if i >= 1:
                    hidden_hi(i - 1)
            for hf in range(HALVES):
                act.wait_ge(mid_ok, hf + 1)
                nc.scalar.activation(mid[:, hf * HB:(hf + 1) * HB, :].rearrange("p b t -> p (b t)"), S[hf][:],
                                     ACT.Gelu).then_inc(midg_ok, 1)

        @block.tensor
        def _(pe):
            pe.wait_ge(ident_ok, 1)
            pe.wait_ge(rows_in, 16 * 8)
            pe.transpose(S[0][:, 0:36], rows[:], ident[0:36, 0:36]).then_inc(rowsT_ok, 1)
            for hf in range(HALVES):
                pe.wait_ge(x_in[hf], 16 * 3)
                for b in range(HB):
                    mm = pe.transpose(Y[hf][:, b * T:(b + 1) * T], x_tok[:, hf * HB + b, :], ident[:])
                mm.then_inc(xT_ok, 1)
            pe.wait_ge(consts_ok, N_CONSTS)
            for b in range(B):
                mm = pe.matmul(S[1][:, 3 * b:3 * b + 3], x_tok[:, b, :], means[:], start=True, stop=True)
            mm.then_inc(pooled_ok, 1)
            pe.wait_ge(cn_ok, 1)
            pe.transpose(S[2][:, 0:8], cn[:], ident[0:8, 0:8]).then_inc(cnT_ok, 1)

            def z_product(i):
                hf, e, c, _ = unit(i)
                lo, hi = SPAN[e]
                n = hi - lo
                if c == 0:
                    wait_split(pe, 2 * ORDER.index(e))
                    pe.wait_ge(x_split, 2 * (hf + 1))
                if i >= NZ:
                    pe.wait_ge(h_ok, i - NZ + 1)
                o = Z[i % NZ][:, 0:HB * n].rearrange("p (b t) -> p b t", b=HB)
                xs = slice(hf * HB, (hf + 1) * HB)
                ws = slice(c * 128, (c + 1) * 128)
                pe.matmul(o, w1_hi[:, e, ws], x_hi[:, xs, lo:hi], start=True, stop=False)
                pe.matmul(o, w1_hi[:, e, ws], x_lo[:, xs, lo:hi], start=False, stop=False)
                pe.matmul(o, w1_lo[:, e, ws], x_hi[:, xs, lo:hi], start=False, stop=True).then_inc(z_ok, 1)

            def y_product(i):
                _, e, c, u = unit(i)
                lo, hi = SPAN[e]
                n = HB * (hi - lo)
                if c == 0:
                    wait_split(pe, 2 * ORDER.index(e) + 1)
                    if u < 2:
                        pe.wait_ge(xT_copied, HALVES)
                    else:
                        pe.wait_ge(acc_ok, u - 1)
                pe.wait_ge(lo_ok, i + 1)
                o = Y[u % 2][:, 0:n]
                s = i % NH
                pe.matmul(o, w2_hi[:, e, c, :], h_hi[:, s, 0:n], start=(c == 0), stop=False)
                pe.matmul(o, w2_lo[:, e, c, :], h_hi[:, s, 0:n], start=False, stop=False)
                pe.matmul(o, w2_hi[:, e, c, :], h_lo[:, s, 0:n], start=False, stop=(c == NC - 1)).then_inc(y_ok, 1)

            def logits():
                pe.wait_ge(gate_in, 16 * 4)
                pe.wait_ge(cols_ok, 1)
                pe.wait_ge(sil_step, 3)
                pe.matmul(S[0][0:8, 8:8 + 2 * E], sil[:, 3, :], tw[:], start=True, stop=False)
                pe.matmul(S[0][0:8, 8:8 + 2 * E], ones[0:1, 0:8], gtb[:, E:3 * E], start=False, stop=True)
                pe.wait_ge(pooled_copied, 1)
                for k in range(3):
                    pe.matmul(S[0][0:8, 0:E], pooled[:, :, k], gw[:, k, :], start=(k == 0), stop=False)
                pe.matmul(S[0][0:8, 0:E], ones[0:1, 0:8], gtb[:, 0:E], start=False, stop=True).then_inc(logit_ok, 1)

            def cond_hidden():
                pe.wait_ge(base_in, 16 * 4)
                pe.wait_ge(cT_step, 1)
                pe.matmul(S[2][:, 16:24], W1_s[:], cT[:], start=True, stop=True).then_inc(hpre_ok, 1)

            def spread_weights():
                pe.wait_ge(wdiag_ok, 1)
                pe.matmul(S[1][:, 32:64], ones[0:8, :], wdiag[:].rearrange("p b e -> p (b e)"),
                          start=True, stop=True).then_inc(wbc_ok, 1)

            def up_turned():
                pe.wait_ge(nmax_ok, 1)
                pe.transpose(S[0][:, 128:256], up[:], ident[:]).then_inc(upT_ok, 1)

            def adaptive():
                pe.wait_ge(hc_ok, 1)
                pe.wait_ge(W2_in, 32)
                wv = W2_s[:].rearrange("p (q d r) -> p q d r", q=Q, r=R)
                for q in range(Q):
                    for r in range(R):
                        c = (q * R + r) * B
                        mm = pe.matmul(S[2][:, c:c + B], wv[:, q, :, r], hc[:], start=True, stop=True)
                mm.then_inc(adapt_ok, 1)

            def adaptive_turned():
                pe.wait_ge(lr_ok, 1)
                pe.wait_ge(upT_copied, 1)
                for q in range(Q):
                    mm = pe.transpose(S[0][0:64, q * 128:(q + 1) * 128], lr[:, q, :], ident[:])
                mm.then_inc(lT_ok, 1)

            def merge(m):
                hf, kind = m % 2, m // 2
                rr = slice(hf * HB * R, (hf + 1) * HB * R)
                pe.wait_ge(lT_copied, 3)
                if m >= 2:
                    pe.wait_ge(merged, m - 1)
                else:
                    pe.wait_ge(wbc_copied, 1)
                pe.matmul(S[1 + m % 2][:], lT[rr, kind, :], lM[rr, kind].rearrange("p b n -> p (b n)"),
                          start=True, stop=True).then_inc(merge_ok, 1)

            def mid_product(hf):
                if hf == 1:
                    pe.wait_ge(merged, 4)
                for b in range(hf * HB, (hf + 1) * HB):
                    j = b % HB
                    mm = pe.matmul(S[hf][:, j * T:(j + 1) * T], WM[:, b, :], acc[:, b, :], start=True, stop=True)
                mm.then_inc(mid_ok, 1)

            out_bank = (S[2], Z[0])

            def out_residual(hf):
                for b in range(hf * HB, (hf + 1) * HB):
                    j = b % HB
                    pe.matmul(out_bank[hf][:, j * D:(j + 1) * D], acc[:, b, :], two_i[:], start=(j == 0), stop=False,
                              skip_group_check=True)

            def out_product(hf):
                pe.wait_ge(midg_ok, hf + 1)
                for b in range(hf * HB, (hf + 1) * HB):
                    j = b % HB
                    mm = pe.matmul(out_bank[hf][:, j * D:(j + 1) * D], mid[:, b, :], WO[:, b, :], start=False,
                                   stop=(j == HB - 1), skip_group_check=True)
                mm.then_inc(o_ok, 1)

            side = {0: [logits], 2: [spread_weights, cond_hidden], 3: [up_turned], 6: [adaptive], 9: [adaptive_turned],
                    11: [lambda: merge(0)], 12: [lambda: merge(1)], 13: [lambda: merge(2)], 14: [lambda: merge(3)]}
            for i in range(CHUNKS + LAG):
                for job in side.get(i, []):
                    job()
                if i < CHUNKS:
                    z_product(i)
                if i >= LAG:
                    y_product(i - LAG)
            pe.wait_ge(merged, 4)
            pe.wait_ge(acc_ok, NE)
            mid_product(0)
            out_residual(0)
            pe.wait_ge(acc_ok, 2 * NE)
            mid_product(1)
            out_residual(1)
            out_product(0)
            out_product(1)

        @block.vector
        def _(dve):
            def split(dst_hi, dst_lo, src, hi_sem, hi_count, lo_sem):
                nc.vector.tensor_copy(dst_hi, src).then_inc(hi_sem, 1)
                dve.wait_ge(hi_sem, hi_count)
                nc.vector.tensor_tensor(dst_lo, src, dst_hi.bitcast(F32), ALU.subtract).then_inc(lo_sem, 1)

            def weight_hi(k):
                raw, hi, _, landed = w_parts(k)
                dve.wait_ge(landed, 16)
                nc.vector.tensor_copy(hi, raw).then_inc(w_hi_ok, 1)

            def weight_split(k):
                raw, hi, lo, landed = w_parts(k)
                dve.wait_ge(landed, 16)
                split(hi, lo, raw, w_hi_ok, k + 1, w_lo_ok)

            def x_half(hf):
                xs = slice(hf * HB, (hf + 1) * HB)
                dve.wait_ge(xT_copied, hf + 1)
                split(x_hi[:, xs, :], x_lo[:, xs, :], xT[:, xs, :], x_split, 2 * hf + 1, x_split)

            def layer_norm():
                dve.wait_ge(rows_in, 16 * 8)
                nc.vector.bn_stats(stats[:], rows[0:8, :]).then_inc(ln_step, 1)
                dve.wait_ge(ln_step, 1)
                nc.vector.bn_aggr(mv[:, 0:2], stats[:]).then_inc(ln_step, 1)
                dve.wait_ge(ln_step, 2)
                nc.vector.tensor_scalar(mv[:, 2:3], mv[:, 1:2], EPS, None, ALU.add).then_inc(ln_step, 1)

            def normed():
                dve.wait_ge(rstd_ok, 1)
                nc.vector.tensor_scalar(cn[:], rows[0:8, :], mv[:, 0:1], mv[:, 3:4], ALU.subtract,
                                        ALU.mult).then_inc(cn_ok, 1)

            def silu():
                dve.wait_ge(exp_sil, 1)
                nc.vector.tensor_scalar(sil[:, 1, :], sil[:, 0, :], 1.0, None, ALU.add).then_inc(sil_step, 1)
                dve.wait_ge(sil_step, 1)
                nc.vector.reciprocal(sil[:, 2, :], sil[:, 1, :]).then_inc(sil_step, 1)
                dve.wait_ge(sil_step, 2)
                nc.vector.tensor_tensor(sil[:, 3, :], sil[:, 2, :], cols[:, 0:8], ALU.mult).then_inc(sil_step, 1)

            def affine_cond():
                dve.wait_ge(cnT_ok, 1)
                dve.wait_ge(cols_ok, 1)
                nc.vector.tensor_scalar(cT[:], S[2][:, 0:8], cols[:, GAMMA:GAMMA + 1], cols[:, BETA:BETA + 1],
                                        ALU.mult, ALU.add).then_inc(cT_step, 1)

            def gate_logits():
                dve.wait_ge(logit_ok, 1)
                nc.vector.tensor_copy(mod_s[:], S[0][0:8, 8:8 + 2 * E]).then_inc(gate_step, 1)
                dve.wait_ge(gate_step, 1)
                nc.vector.scalar_tensor_tensor(out=lg[:, 0, :], in0=mod_s[:, 0:E], scalar=1.0, in1=S[0][0:8, 0:E],
                                               op0=ALU.add, op1=ALU.mult).then_inc(gate_step, 1)
                dve.wait_ge(gate_step, 2)
                nc.vector.tensor_tensor(lg[:, 1, :], lg[:, 0, :], mod_s[:, E:2 * E], ALU.add).then_inc(gate_step, 1)
                dve.wait_ge(gate_step, 3)
                nc.vector.tensor_reduce(sc[:, 0:1], lg[:, 1, :], AX.X, ALU.max, negate=True).then_inc(nmax_ok, 1)

            def gate_weights():
                dve.wait_ge(exp_ok, 1)
                nc.vector.reciprocal(sc[:, 2:3], sc[:, 1:2]).then_inc(gate_step, 1)
                dve.wait_ge(gate_step, 4)
                nc.vector.tensor_scalar(lg[:, 3, :], lg[:, 2, :], sc[:, 2:3], None, ALU.mult).then_inc(gate_step, 1)
                dve.wait_ge(gate_step, 5)
                p_j = lg[:, 3, :].unsqueeze(1).broadcast_to([8, E, E])
                p_e = lg[:, 3, :].unsqueeze(2).broadcast_to([8, E, E])
                nc.vector.tensor_tensor(cmp[:, :, 0, :], p_j, p_e, ALU.is_ge).then_inc(gate_step, 1)
                nc.vector.tensor_tensor(cmp[:, :, 1, :], p_j, p_e, ALU.is_gt).then_inc(gate_step, 1)
                dve.wait_ge(gate_step, 7)
                dve.wait_ge(consts_ok, N_CONSTS)
                nc.vector.tensor_tensor(cmpm[:], cmp[:], order_mask[:], ALU.mult).then_inc(gate_step, 1)
                dve.wait_ge(gate_step, 8)
                nc.vector.tensor_reduce(lg[:, 4, :], cmpm[:].rearrange("p e t j -> p e (t j)"), AX.X,
                                        ALU.add).then_inc(gate_step, 1)
                dve.wait_ge(gate_step, 9)
                nc.vector.scalar_tensor_tensor(out=lg[:, 5, :], in0=lg[:, 4, :], scalar=1.5, in1=lg[:, 3, :],
                                               op0=ALU.is_lt, op1=ALU.mult,
                                               accum_out=sc[:, 3:4]).then_inc(gate_step, 1)
                dve.wait_ge(gate_step, 10)
                nc.vector.tensor_scalar(sc[:, 4:5], sc[:, 3:4], 1e-8, None, ALU.add).then_inc(gate_step, 1)
                dve.wait_ge(gate_step, 11)
                nc.vector.reciprocal(sc[:, 5:6], sc[:, 4:5]).then_inc(gate_step, 1)
                dve.wait_ge(gate_step, 12)
                nc.vector.tensor_scalar(lg[:, 6, :], lg[:, 5, :], sc[:, 5:6], None, ALU.mult).then_inc(gate_step, 1)
                dve.wait_ge(gate_step, 13)
                nc.vector.tensor_tensor(wdiag[:], lg[:, 6, :].unsqueeze(1).broadcast_to([8, B, E]),
                                        ident[0:8, 0:8].unsqueeze(2).broadcast_to([8, B, E]),
                                        ALU.mult).then_inc(wdiag_ok, 1)

            def region_bias():
                def w(e):
                    return wbc[:, :, e]

                def bias(e):
                    return cols[:, EB2 + e:EB2 + e + 1]

                dve.wait_ge(wbc_ok, 1)
                nc.vector.tensor_copy(wbc[:].rearrange("p b e -> p (b e)"), S[1][:, 32:64]).then_inc(wbc_copied, 1)
                dve.wait_ge(wbc_copied, 1)
                nc.vector.tensor_scalar(br[:, 3, :], w(0), bias(0), bias(SHARED), ALU.mult, ALU.add).then_inc(br_step, 1)
                dve.wait_ge(br_step, 1)
                nc.vector.scalar_tensor_tensor(out=br[:, 4, :], in0=w(3), scalar=bias(3), in1=br[:, 3, :],
                                               op0=ALU.mult, op1=ALU.add).then_inc(br_step, 1)
                dve.wait_ge(br_step, 2)
                nc.vector.scalar_tensor_tensor(out=br[:, 0, :], in0=w(1), scalar=bias(1), in1=br[:, 4, :],
                                               op0=ALU.mult, op1=ALU.add).then_inc(br_step, 1)
                nc.vector.scalar_tensor_tensor(out=br[:, 2, :], in0=w(2), scalar=bias(2), in1=br[:, 4, :],
                                               op0=ALU.mult, op1=ALU.add).then_inc(br_step, 1)
                dve.wait_ge(br_step, 4)
                nc.vector.scalar_tensor_tensor(out=br[:, 1, :], in0=w(2), scalar=bias(2), in1=br[:, 0, :],
                                               op0=ALU.mult, op1=ALU.add).then_inc(br_step, 1)

            def x_plus_bias(hf):
                xs = slice(hf * HB, (hf + 1) * HB)
                dve.wait_ge(br_step, 5)
                for g, (_, p0, n) in enumerate(REGIONS):
                    nc.vector.tensor_tensor(acc[:, xs, p0:p0 + n], xT[:, xs, p0:p0 + n],
                                            br[:, g, xs].unsqueeze(2).broadcast_to([128, HB, n]),
                                            ALU.add).then_inc(xb_ok, 1)

            def hidden_lo(i):
                _, e, _, _ = unit(i)
                lo, hi = SPAN[e]
                n = HB * (hi - lo)
                s = i % NH
                dve.wait_ge(hi_ok, i + 1)
                if i >= NH:
                    dve.wait_ge(y_ok, i - NH + 1)
                nc.vector.tensor_tensor(h_lo[:, s, 0:n], h[:, s, 0:n], h_hi[:, s, 0:n].bitcast(F32),
                                        ALU.subtract).then_inc(lo_ok, 1)

            def accumulate(u):
                hf, e = u // NE, ORDER[u % NE]
                lo, hi = SPAN[e]
                n = hi - lo
                dve.wait_ge(y_ok, NC * (u + 1))
                y = Y[u % 2]
                if e == SHARED:
                    xs = slice(hf * HB, (hf + 1) * HB)
                    dve.wait_ge(xb_ok, 3 * (hf + 1))
                    a = acc[:, xs, :].rearrange("p b t -> p (b t)")
                    nc.vector.tensor_tensor(a, y[:], a, ALU.add).then_inc(acc_ok, 1)
                    return
                dve.wait_ge(acc_ok, u)
                for j in range(HB):
                    b = hf * HB + j
                    ins = nc.vector.scalar_tensor_tensor(
                        out=acc[:, b, lo:hi], in0=y[:, j * n:(j + 1) * n], scalar=wbc[:, b, e:e + 1],
                        in1=acc[:, b, lo:hi], op0=ALU.mult, op1=ALU.add)
                ins.then_inc(acc_ok, 1)

            def up_copied():
                dve.wait_ge(upT_ok, 1)
                nc.vector.tensor_copy(upT[:], S[0][:, 128:256]).then_inc(upT_copied, 1)

            def adaptive_biased():
                dve.wait_ge(adapt_ok, 1)
                dve.wait_ge(base_in, 16 * 4)
                for q in range(Q):
                    ins = nc.vector.tensor_tensor(
                        lr[:, q, :].rearrange("p (b r) -> p b r", r=R),
                        S[2][:, q * R * B:(q + 1) * R * B].rearrange("p (r b) -> p b r", b=B),
                        b2c[:, q, :].unsqueeze(1).broadcast_to([128, B, R]), ALU.add)
                ins.then_inc(lr_ok, 1)

            def adaptive_spread():
                dve.wait_ge(lT_ok, 1)
                dve.wait_ge(consts_ok, N_CONSTS)
                t = S[0][0:64, :].rearrange("p (q n) -> p q n", q=Q)
                nc.vector.tensor_copy(lT[:, 0, :], t[:, 2, :]).then_inc(lT_copied, 1)
                nc.vector.tensor_copy(lT[:, 1, :], t[:, 1, :]).then_inc(lT_copied, 1)
                for k, q in ((0, 3), (1, 0)):
                    ins = nc.vector.tensor_tensor(lM[:, k], t[:, q, :].unsqueeze(1).broadcast_to([64, HB, 128]),
                                                  own[:].unsqueeze(2).broadcast_to([64, HB, 128]), ALU.mult)
                ins.then_inc(lT_copied, 1)

            def merge_out(m):
                hf, kind = m % 2, m // 2
                dst, base = ((WM, down), (WO, upT))[kind]
                dve.wait_ge(merge_ok, m + 1)
                if m == 2:
                    dve.wait_ge(upT_copied, 1)
                nc.vector.tensor_tensor(dst[:, hf * HB:(hf + 1) * HB, :],
                                        S[1 + m % 2][:].rearrange("p (b n) -> p b n", b=HB),
                                        base[:].unsqueeze(1).broadcast_to([128, HB, 128]),
                                        ALU.add).then_inc(merged, 1)

            def store_half(hf):
                dve.wait_ge(o_ok, hf + 1)
                src = (S[2], Z[0])[hf]
                nc.vector.tensor_copy(o_tok[:, hf * HB:(hf + 1) * HB, :].rearrange("p b d -> p (b d)"),
                                      src[:]).then_inc(o_copied, 1)

            layer_norm()
            normed()
            silu()
            affine_cond()
            x_half(0)
            weight_split(0)
            dve.wait_ge(pooled_ok, 1)
            nc.vector.tensor_copy(pooled[:].rearrange("p b k -> p (b k)"), S[1][:, 0:24]).then_inc(pooled_copied, 1)
            gate_logits()
            weight_split(1)
            gate_weights()
            weight_hi(2)
            weight_hi(3)
            side = {0: [lambda: weight_hi(4)], 1: [lambda: weight_hi(5)], 2: [region_bias, lambda: x_plus_bias(0)],
                    3: [up_copied], 4: [lambda: weight_hi(6)], 5: [lambda: weight_hi(7)],
                    7: [adaptive_biased, lambda: weight_hi(8)], 8: [lambda: weight_hi(9)], 9: [adaptive_spread],
                    10: [lambda: x_half(1)], 11: [lambda: merge_out(0)], 12: [lambda: merge_out(1)],
                    13: [lambda: merge_out(2)], 14: [lambda: merge_out(3)], 15: [lambda: x_plus_bias(1)]}
            for i in range(CHUNKS + LAG + 1):
                if i < CHUNKS:
                    hidden_lo(i)
                for job in side.get(i, []):
                    job()
                last = i - LAG - 1
                if last >= 0 and last % NC == NC - 1:
                    accumulate(last // NC)
            store_half(0)
            store_half(1)


_INS = ["x", "cond_1024", "L0_cond_gate_w", "L0_cond_gate_b", "L0_cond_time_w", "L0_cond_time_b", "L0_cond_ew1",
        "L0_cond_eb1", "L0_cond_ew2", "L0_cond_eb2", "L0_cond_sw1", "L0_cond_sb1", "L0_cond_sw2", "L0_cond_sb2",
        "L1_cond_base_up", "L1_cond_base_down", "L1_cond_ln_gamma", "L1_cond_ln_beta", "L1_cond_W1", "L1_cond_bias1",
        "L1_cond_W2", "L1_cond_bias2"]


def kernel(**inputs):
    import numpy as _np
    import concourse.bacc as _bacc
    from concourse import mybir as _mybir
    from concourse.bass_utils import run_bass_kernel_spmd as _run

    nc = _bacc.Bacc("TRN2", target_bir_lowering=False, num_devices=1)
    arrays, args = {}, []
    for name in _INS:
        a = _np.ascontiguousarray(inputs[name])
        arrays[f"in_{name}_dram"] = a
        args.append(nc.dram_tensor(f"in_{name}_dram", a.shape, _mybir.dt.from_np(a.dtype), kind="ExternalInput").ap())
    xs = inputs["x"]
    out = nc.dram_tensor("out_0_dram", xs.shape, _mybir.dt.from_np(_np.dtype("float32")), kind="ExternalOutput").ap()
    moe_lowrank_kernel(nc, *args, out)
    r = _run(nc, [arrays], core_ids=[0])
    return r.results[0]["out_0_dram"]
```

```python
from contextlib import ExitStack

import concourse.bass as bass
from concourse import mybir

ALU = mybir.AluOpType
ACT = mybir.ActivationFunctionType
AX = mybir.AxisListType
F32 = mybir.dt.float32
F32R = mybir.dt.float32r

EPS = 1e-5


def regions(T):
    third = T // 3
    rest = T - 2 * third
    return (0, 0, third), (2 * third, third, rest), (third, third + rest, third)


def moe_lowrank_kernel(nc, xT_d, w_d, cols_d, rows_d, base_d, W2_d, b2_d, out_d):
    D, B, T = xT_d.shape
    NE = w_d.shape[0]
    E = NE - 1
    SHARED = E
    NC = w_d.shape[2] // (2 * D)
    H = NC * 128
    R, QD = b2_d.shape
    Q = QD // D
    REGIONS = regions(T)
    HEAD, PROP = REGIONS[0][2], REGIONS[1][2]
    SPAN = {0: (0, T), 1: (0, HEAD + PROP), 2: (HEAD, T), 3: (0, T), SHARED: (0, T)}
    HALVES = 2
    HB = B // HALVES
    ORDER = (SHARED, 0, 3, 1, 2)
    CHUNKS = HALVES * NE * NC
    LAG = 3
    NZ, NH = 3, 5
    HALF_ROWS = HB * R
    STEP = 128 + HB

    def unit(i):
        u = i // NC
        return u // NE, ORDER[u % NE], i % NC, u

    with ExitStack() as ctx:
        def sb(name, shape, dt=F32):
            return ctx.enter_context(nc.sbuf_tensor(name, shape, dt))

        def pb(name):
            return ctx.enter_context(nc.psum_tensor(name, [128, 512], F32))

        def sem(name):
            return ctx.enter_context(nc.semaphore(name))

        xT = sb("xT", [128, B, T])
        w = sb("w", [128, NE, 2, H])
        cols = sb("cols", [128, cols_d.shape[1]])
        rows = sb("rows", [8, rows_d.shape[1]])
        base = sb("base", [128, 3, 128])
        W2 = sb("W2", [128, R, QD])
        b2 = sb("b2", [2 * HALF_ROWS, QD])
        EB1 = B
        EB2 = EB1 + NE * NC
        BIAS1 = EB2 + NE
        GAMMA, BETA = BIAS1 + 1, BIAS1 + 2
        GW = BETA + 1
        TW = GW + 3 * E
        OWN = TW + 2 * E
        condT = cols[:, 0:B]
        gw = cols[:, GW:TW].rearrange("p (k e) -> p k e", k=3)
        tw = cols[:, TW:OWN]
        own = cols[0:2 * HALF_ROWS, OWN:OWN + HB]
        cond = rows[:, 0:128]
        gate_b = rows[0:1, 128:128 + E]
        time_b = rows[0:1, 128 + E:128 + 3 * E]
        ident = rows[:, 128 + 3 * E:128 + 3 * E + 8]
        order_mask = rows[:, 136 + 3 * E:136 + 3 * E + 2 * E * E].rearrange("p (e t j) -> p e t j", e=E, t=2)
        down, upT, W1 = base[:, 0, :], base[:, 1, :], base[:, 2, :]
        w_hi, w_lo = sb("w_hi", [128, NE, 2, H], F32R), sb("w_lo", [128, NE, 2, H], F32R)
        x_hi, x_lo = sb("x_hi", [128, B, T], F32R), sb("x_lo", [128, B, T], F32R)
        W2_hi, W2_lo = sb("W2_hi", [128, R, QD], F32R), sb("W2_lo", [128, R, QD], F32R)
        wide = sb("wide", [128, R * STEP], F32R)
        h = sb("h", [128, NH, 512])
        h_hi, h_lo = sb("h_hi", [128, NH, 512], F32R), sb("h_lo", [128, NH, 512], F32R)
        acc = sb("acc", [128, B, T])
        mid = sb("mid", [128, B, T])
        oT = sb("oT", [128, B, T])
        ones = sb("ones", [8, 128])
        sums = sb("sums", [128, 3, B])
        joint = sb("joint", [128, 3, B])
        pooled = sb("pooled", [128, 3, B])
        sil = sb("sil", [128, 4, B])
        mod_s = sb("mod_s", [8, 2 * E])
        lg = sb("lg", [8, 7, E])
        sc = sb("sc", [8, 6])
        cmp = sb("cmp", [8, E, 2, E])
        cmpm = sb("cmpm", [8, E, 2, E])
        wdiag = sb("wdiag", [8, B, E])
        wbc = sb("wbc", [128, B, E])
        br = sb("br", [128, 5, B])
        half_neg = sb("half_neg", [8, 1])
        stats = sb("stats", [8, 6])
        mv = sb("mv", [8, 4])
        cn = sb("cn", [8, 128])
        cT = sb("cT", [128, B])
        hc = sb("hc", [128, B])
        part = sb("part", [2 * HALF_ROWS, QD])
        lr = sb("lr", [2 * HALF_ROWS, Q, D])
        spread = sb("spread", [2 * HALF_ROWS, 2, HB, D])
        WM = sb("WM", [128, B, 128])
        WO = sb("WO", [128, B, 128])

        Z = [pb(f"Z{i}") for i in range(NZ)]
        Y = [pb(f"Y{i}") for i in range(2)]
        S = [pb(f"S{i}") for i in range(3)]

        x_in = [sem(f"x_in{i}") for i in range(HALVES)]
        w_in = [sem(f"w_in{k}") for k in range(2 * NE)]
        cols_in = sem("cols_in")
        rows_in = sem("rows_in")
        base_in = sem("base_in")
        W2_in = [sem(f"W2_in{c}") for c in range(2)]
        b2_in = sem("b2_in")
        out_done = sem("out_done")
        consts_ok = sem("consts_ok")
        rstd_ok = sem("rstd_ok")
        w_lo_pool = sem("w_lo_pool")
        W2_lo_ok = sem("W2_lo_ok")
        spread_ok = sem("spread_ok")
        cnT_ok = sem("cnT_ok")
        hpre_ok = sem("hpre_ok")
        logit_ok = sem("logit_ok")
        wbc_ok = sem("wbc_ok")
        adapt_ok = sem("adapt_ok")
        merge_ok = sem("merge_ok")
        z_ok = sem("z_ok")
        y_ok = sem("y_ok")
        mid_ok = sem("mid_ok")
        o_ok = sem("o_ok")
        exp_sil = sem("exp_sil")
        x0_hi = sem("x0_hi")
        w0_hi = sem("w0_hi")
        hc_ok = sem("hc_ok")
        exp_ok = sem("exp_ok")
        h_ok = sem("h_ok")
        hi_ok = sem("hi_ok")
        midg_ok = sem("midg_ok")
        ln_step = sem("ln_step")
        cn_ok = sem("cn_ok")
        cT_ok = sem("cT_ok")
        x1_hi = sem("x1_hi")
        x_lo_ok = sem("x_lo_ok")
        w_hi_ok = sem("w_hi_ok")
        w_lo_ok = sem("w_lo_ok")
        W2_hi_ok = sem("W2_hi_ok")
        pool_step = sem("pool_step")
        sil_step = sem("sil_step")
        gate_step = sem("gate_step")
        nmax_ok = sem("nmax_ok")
        wdiag_ok = sem("wdiag_ok")
        wbc_copied = sem("wbc_copied")
        br_step = sem("br_step")
        xb_ok = sem("xb_ok")
        wide_ok = sem("wide_ok")
        part_ok = sem("part_ok")
        lr_ok = sem("lr_ok")
        merged = sem("merged")
        lo_ok = sem("lo_ok")
        acc_ok = sem("acc_ok")
        acc_early = sem("acc_early")
        o_copied = sem("o_copied")

        DVE_LO = 2

        def w_part(tile, k):
            return tile[:, ORDER[k // 2], k % 2, :]

        def wait_split(eng, k):
            if k < DVE_LO:
                eng.wait_ge(w_lo_ok, k + 1)
            else:
                eng.wait_ge(w_lo_pool, k - DVE_LO + 1)

        def half(hf):
            return slice(hf * HB, (hf + 1) * HB)

        PIECES = ((0, HB), (HB, HB + HB // 2), (HB + HB // 2, B))
        MID_BANK = (S[0], S[1], Z[0])
        OUT_BANK = (S[2], Z[1], Z[2])

        block = ctx.enter_context(nc.Block())

        @block.sync
        def _(sp):
            def load_w(k):
                e, f = ORDER[k // 2], k % 2
                sp.dma_start(w[:, e, f, :], w_d[e, :, f * H:(f + 1) * H]).then_inc(w_in[k], 16)

            sp.dma_start(xT[:, half(0), :], xT_d[:, half(0), :]).then_inc(x_in[0], 16)
            load_w(0)
            sp.dma_start(rows[:], rows_d).then_inc(rows_in, 16)
            sp.dma_start(cols[:], cols_d).then_inc(cols_in, 16)
            sp.dma_start(base[:], base_d).then_inc(base_in, 16)
            sp.dma_start(xT[:, half(1), :], xT_d[:, half(1), :]).then_inc(x_in[1], 16)
            for k in range(1, 2 * NE):
                load_w(k)
                if k == 5:
                    for c in range(2):
                        rs = slice(c * R // 2, (c + 1) * R // 2)
                        sp.dma_start(W2[:, rs, :], W2_d[:, rs, :]).then_inc(W2_in[c], 16)
            for hf in range(HALVES):
                sp.dma_start(b2[hf * HALF_ROWS:(hf + 1) * HALF_ROWS, :],
                             b2_d.unsqueeze(1).broadcast_to([R, HB, QD])).then_inc(b2_in, 16)
            for n, (b0, b1) in enumerate(PIECES):
                sp.wait_ge(o_copied, n + 1)
                sp.dma_start(out_d[:, b0:b1, :], oT[:, b0:b1, :]).then_inc(out_done, 16)
            sp.wait_ge(out_done, 16 * len(PIECES))

        @block.gpsimd
        def _(pool):
            pool.memset(half_neg[:], -0.5).then_inc(consts_ok, 1)
            pool.memset(ones[:], 1.0).then_inc(consts_ok, 1)
            pool.memset(wide[:].bitcast(F32), 0.0).then_inc(consts_ok, 1)
            pool.wait_ge(ln_step, 3)
            pool.wait_ge(consts_ok, 1)
            pool.tensor_tensor(mv[:, 3:4], mv[:, 2:3], half_neg[:], ALU.pow).then_inc(rstd_ok, 1)
            for k in range(DVE_LO, 2 * NE):
                pool.wait_ge(w_hi_ok, k)
                pool.tensor_tensor(w_part(w_lo, k), w_part(w, k), w_part(w_hi, k).bitcast(F32),
                                   ALU.subtract).then_inc(w_lo_pool, 1)
            for r in range(R):
                pool.wait_ge(W2_hi_ok, r + 1)
                pool.tensor_tensor(W2_lo[:, r, :], W2[:, r, :], W2_hi[:, r, :].bitcast(F32),
                                   ALU.subtract).then_inc(W2_lo_ok, 1)
            pool.wait_ge(lr_ok, 1)
            for k, q in ((0, 3), (1, 0)):
                pool.tensor_tensor(spread[:, k], lr[:, q, :].unsqueeze(1).broadcast_to([2 * HALF_ROWS, HB, D]),
                                   own.unsqueeze(2).broadcast_to([2 * HALF_ROWS, HB, D]),
                                   ALU.mult).then_inc(spread_ok, 1)

        @block.scalar
        def _(act):
            act.wait_ge(cols_in, 16)
            nc.scalar.activation(sil[:, 0, :], condT, ACT.Exp, scale=-1.0).then_inc(exp_sil, 1)
            act.wait_ge(x_in[0], 16)
            nc.scalar.activation(x_hi[:, half(0), :], xT[:, half(0), :], ACT.Copy).then_inc(x0_hi, 1)
            act.wait_ge(w_in[0], 16)
            nc.scalar.activation(w_part(w_hi, 0), w_part(w, 0), ACT.Copy).then_inc(w0_hi, 1)
            act.wait_ge(hpre_ok, 1)
            nc.scalar.activation(hc[:], S[2][:, 0:B], ACT.Gelu, bias=cols[:, BIAS1:BIAS1 + 1]).then_inc(hc_ok, 1)
            act.wait_ge(nmax_ok, 1)
            nc.scalar.activation(lg[:, 2, :], lg[:, 1, :], ACT.Exp, bias=sc[:, 0:1],
                                 accum_out=sc[:, 1:2]).then_inc(exp_ok, 1)

            def gelu(i):
                _, e, c, _ = unit(i)
                lo, hi = SPAN[e]
                n = HB * (hi - lo)
                act.wait_ge(z_ok, i + 1)
                if i >= NH:
                    act.wait_ge(lo_ok, i - NH + 1)
                b = EB1 + e * NC + c
                nc.scalar.activation(h[:, i % NH, 0:n], Z[i % NZ][:, 0:n], ACT.Gelu_apprx_tanh,
                                     bias=cols[:, b:b + 1]).then_inc(h_ok, 1)

            def hidden_hi(i):
                _, e, _, _ = unit(i)
                lo, hi = SPAN[e]
                n = HB * (hi - lo)
                act.wait_ge(h_ok, i + 1)
                if i >= NH:
                    act.wait_ge(y_ok, i - NH + 1)
                nc.scalar.activation(h_hi[:, i % NH, 0:n], h[:, i % NH, 0:n], ACT.Copy).then_inc(hi_ok, 1)

            for i in range(CHUNKS + 1):
                if i < CHUNKS:
                    gelu(i)
                if i >= 1:
                    hidden_hi(i - 1)
            for n, (b0, b1) in enumerate(PIECES):
                act.wait_ge(mid_ok, n + 1)
                nc.scalar.activation(mid[:, b0:b1, :].rearrange("p b t -> p (b t)"),
                                     MID_BANK[n][:, 0:(b1 - b0) * T], ACT.Gelu).then_inc(midg_ok, 1)

        @block.tensor
        def _(pe):
            def cond_turned():
                pe.wait_ge(rows_in, 16)
                pe.wait_ge(cn_ok, 1)
                pe.transpose(S[1][:, 0:B], cn[:], ident).then_inc(cnT_ok, 1)

            def cond_hidden():
                pe.wait_ge(base_in, 16)
                pe.wait_ge(cT_ok, 1)
                pe.matmul(S[2][:, 0:B], W1, cT[:], start=True, stop=True).then_inc(hpre_ok, 1)

            def z_product(i):
                hf, e, c, _ = unit(i)
                lo, hi = SPAN[e]
                n = hi - lo
                if c == 0:
                    wait_split(pe, 2 * ORDER.index(e))
                    pe.wait_ge(x_lo_ok, hf + 1)
                if i >= NZ:
                    pe.wait_ge(h_ok, i - NZ + 1)
                o = Z[i % NZ][:, 0:HB * n].rearrange("p (b t) -> p b t", b=HB)
                xs = half(hf)
                ws = slice(c * 128, (c + 1) * 128)
                pe.matmul(o, w_hi[:, e, 0, ws], x_hi[:, xs, lo:hi], start=True, stop=False)
                pe.matmul(o, w_hi[:, e, 0, ws], x_lo[:, xs, lo:hi], start=False, stop=False)
                pe.matmul(o, w_lo[:, e, 0, ws], x_hi[:, xs, lo:hi], start=False, stop=True).then_inc(z_ok, 1)

            def y_product(i):
                _, e, c, u = unit(i)
                lo, hi = SPAN[e]
                n = HB * (hi - lo)
                if c == 0:
                    wait_split(pe, 2 * ORDER.index(e) + 1)
                    if u >= 2:
                        pe.wait_ge(acc_ok, u - 1)
                pe.wait_ge(lo_ok, i + 1)
                o = Y[u % 2][:, 0:n]
                s = i % NH
                ws = slice(c * 128, (c + 1) * 128)
                pe.matmul(o, w_hi[:, e, 1, ws], h_hi[:, s, 0:n], start=(c == 0), stop=False)
                pe.matmul(o, w_lo[:, e, 1, ws], h_hi[:, s, 0:n], start=False, stop=False)
                pe.matmul(o, w_hi[:, e, 1, ws], h_lo[:, s, 0:n], start=False, stop=(c == NC - 1)).then_inc(y_ok, 1)

            def logits():
                pe.wait_ge(consts_ok, 3)
                pe.wait_ge(sil_step, 3)
                pe.matmul(S[0][0:8, 8:8 + 2 * E], sil[:, 3, :], tw, start=True, stop=False)
                pe.matmul(S[0][0:8, 8:8 + 2 * E], ones[0:1, 0:8], time_b, start=False, stop=True)
                pe.wait_ge(pool_step, 7)
                for k in range(3):
                    pe.matmul(S[0][0:8, 0:E], pooled[:, k, :], gw[:, k, :], start=(k == 0), stop=False)
                pe.matmul(S[0][0:8, 0:E], ones[0:1, 0:8], gate_b, start=False, stop=True).then_inc(logit_ok, 1)

            def spread_weights():
                pe.wait_ge(wdiag_ok, 1)
                pe.matmul(S[1][:, 0:B * E], ones[:], wdiag[:].rearrange("p b e -> p (b e)"),
                          start=True, stop=True).then_inc(wbc_ok, 1)

            def adaptive(r0, r1):
                pe.wait_ge(wide_ok, 2)
                pe.wait_ge(nmax_ok, 1)
                for r in range(r0, r1):
                    pe.wait_ge(W2_lo_ok, r + 1)
                    ws = wide[:, r * 128:(r + 1) * 128]
                    pe.matmul(S[0][:], ws, W2_hi[:, r, :], start=(r == 0), stop=False)
                    mm = pe.matmul(S[0][:], ws, W2_lo[:, r, :], start=False, stop=(r == R - 1))
                if r1 == R:
                    mm.then_inc(adapt_ok, 1)

            def merge(m):
                hf, kind = m % 2, m // 2
                rr = slice(hf * HALF_ROWS, (hf + 1) * HALF_ROWS)
                pe.wait_ge(spread_ok, kind + 1)
                if m == 0:
                    pe.wait_ge(wbc_copied, 1)
                elif m == 1:
                    pe.wait_ge(hc_ok, 1)
                else:
                    pe.wait_ge(merged, m - 1)
                pe.matmul(S[1 + m % 2][:], lr[rr, 2 - kind, :], spread[rr, kind].rearrange("p b n -> p (b n)"),
                          start=True, stop=True).then_inc(merge_ok, 1)

            def mid_product(n):
                b0, b1 = PIECES[n]
                if n == 0:
                    pe.wait_ge(acc_ok, NE)
                    pe.wait_ge(lr_ok, 1)
                    pe.wait_ge(merged, 2)
                elif n == 1:
                    pe.wait_ge(acc_early, 1)
                    pe.wait_ge(merged, 3)
                else:
                    pe.wait_ge(acc_ok, HALVES * NE)
                for b in range(b0, b1):
                    j = b - b0
                    mm = pe.matmul(MID_BANK[n][:, j * T:(j + 1) * T], WM[:, b, :], acc[:, b, :], start=True, stop=True)
                mm.then_inc(mid_ok, 1)

            def out_product(n):
                b0, b1 = PIECES[n]
                pe.wait_ge(midg_ok, n + 1)
                pe.wait_ge(merged, 4)
                for b in range(b0, b1):
                    j = b - b0
                    mm = pe.matmul(OUT_BANK[n][:, j * T:(j + 1) * T], WO[:, b, :], mid[:, b, :], start=True, stop=True)
                mm.then_inc(o_ok, 1)

            side = {2: [logits], 4: [spread_weights],
                    20: [lambda: adaptive(0, 2)], 21: [lambda: adaptive(2, 4)],
                    22: [lambda: adaptive(4, 6)], 23: [lambda: adaptive(6, 8)],
                    26: [lambda: merge(0)], 27: [lambda: merge(1)], 28: [lambda: merge(2)], 29: [lambda: merge(3)],
                    32: [lambda: mid_product(0)]}
            cond_turned()
            cond_hidden()
            for i in range(CHUNKS + LAG):
                for job in side.get(i, []):
                    job()
                if i < CHUNKS:
                    z_product(i)
                if i >= LAG:
                    y_product(i - LAG)
            mid_product(1)
            mid_product(2)
            for n in range(len(PIECES)):
                out_product(n)

        @block.vector
        def _(dve):
            def weight_hi(k):
                dve.wait_ge(w_in[k], 16)
                nc.vector.tensor_copy(w_part(w_hi, k), w_part(w, k)).then_inc(w_hi_ok, 1)

            def weight_lo(k):
                if k == 0:
                    dve.wait_ge(w0_hi, 1)
                else:
                    dve.wait_ge(w_hi_ok, k)
                nc.vector.tensor_tensor(w_part(w_lo, k), w_part(w, k), w_part(w_hi, k).bitcast(F32),
                                        ALU.subtract).then_inc(w_lo_ok, 1)

            def x_lo_part(hf):
                xs = half(hf)
                if hf == 0:
                    dve.wait_ge(x0_hi, 1)
                else:
                    dve.wait_ge(x_in[1], 16)
                    nc.vector.tensor_copy(x_hi[:, xs, :], xT[:, xs, :]).then_inc(x1_hi, 1)
                    dve.wait_ge(x1_hi, 1)
                nc.vector.tensor_tensor(x_lo[:, xs, :], xT[:, xs, :], x_hi[:, xs, :].bitcast(F32),
                                        ALU.subtract).then_inc(x_lo_ok, 1)

            def adaptive_hi(r):
                dve.wait_ge(W2_in[r // (R // 2)], 16)
                nc.vector.tensor_copy(W2_hi[:, r, :], W2[:, r, :]).then_inc(W2_hi_ok, 1)

            def layer_norm():
                dve.wait_ge(rows_in, 16)
                nc.vector.bn_stats(stats[:], cond).then_inc(ln_step, 1)
                dve.wait_ge(ln_step, 1)
                nc.vector.bn_aggr(mv[:, 0:2], stats[:]).then_inc(ln_step, 1)
                dve.wait_ge(ln_step, 2)
                nc.vector.tensor_scalar(mv[:, 2:3], mv[:, 1:2], EPS, None, ALU.add).then_inc(ln_step, 1)

            def normed():
                dve.wait_ge(rstd_ok, 1)
                nc.vector.tensor_scalar(cn[:], cond, mv[:, 0:1], mv[:, 3:4], ALU.subtract, ALU.mult).then_inc(cn_ok, 1)

            def affine_cond():
                dve.wait_ge(cols_in, 16)
                dve.wait_ge(cnT_ok, 1)
                nc.vector.tensor_scalar(cT[:], S[1][:, 0:B], cols[:, GAMMA:GAMMA + 1], cols[:, BETA:BETA + 1],
                                        ALU.mult, ALU.add).then_inc(cT_ok, 1)

            def silu():
                dve.wait_ge(exp_sil, 1)
                nc.vector.tensor_scalar(sil[:, 1, :], sil[:, 0, :], 1.0, None, ALU.add).then_inc(sil_step, 1)
                dve.wait_ge(sil_step, 1)
                nc.vector.reciprocal(sil[:, 2, :], sil[:, 1, :]).then_inc(sil_step, 1)
                dve.wait_ge(sil_step, 2)
                nc.vector.tensor_tensor(sil[:, 3, :], sil[:, 2, :], condT, ALU.mult).then_inc(sil_step, 1)

            def pool_tokens():
                dve.wait_ge(x_in[0], 16)
                dve.wait_ge(x_in[1], 16)
                for g, (_, p0, n) in enumerate(REGIONS):
                    nc.vector.tensor_reduce(sums[:, g, :], xT[:, :, p0:p0 + n], AX.X, ALU.add).then_inc(pool_step, 1)
                dve.wait_ge(pool_step, 3)
                nc.vector.tensor_tensor(joint[:, 1:3, :], sums[:, 0:3:2, :],
                                        sums[:, 1, :].unsqueeze(1).broadcast_to([128, 2, B]),
                                        ALU.add).then_inc(pool_step, 1)
                dve.wait_ge(pool_step, 4)
                nc.vector.tensor_tensor(joint[:, 0, :], joint[:, 1, :], sums[:, 2, :], ALU.add).then_inc(pool_step, 1)
                nc.vector.tensor_scalar(pooled[:, 1:3, :], joint[:, 1:3, :], 1.0 / (HEAD + PROP), None,
                                        ALU.mult).then_inc(pool_step, 1)
                dve.wait_ge(pool_step, 6)
                nc.vector.tensor_scalar(pooled[:, 0, :], joint[:, 0, :], 1.0 / T, None, ALU.mult).then_inc(pool_step, 1)

            def gate_logits():
                dve.wait_ge(logit_ok, 1)
                nc.vector.tensor_copy(mod_s[:], S[0][0:8, 8:8 + 2 * E]).then_inc(gate_step, 1)
                dve.wait_ge(gate_step, 1)
                nc.vector.scalar_tensor_tensor(out=lg[:, 0, :], in0=mod_s[:, 0:E], scalar=1.0, in1=S[0][0:8, 0:E],
                                               op0=ALU.add, op1=ALU.mult).then_inc(gate_step, 1)
                dve.wait_ge(gate_step, 2)
                nc.vector.tensor_tensor(lg[:, 1, :], lg[:, 0, :], mod_s[:, E:2 * E], ALU.add).then_inc(gate_step, 1)
                dve.wait_ge(gate_step, 3)
                nc.vector.tensor_reduce(sc[:, 0:1], lg[:, 1, :], AX.X, ALU.max, negate=True).then_inc(nmax_ok, 1)

            def gate_weights():
                dve.wait_ge(exp_ok, 1)
                nc.vector.reciprocal(sc[:, 2:3], sc[:, 1:2]).then_inc(gate_step, 1)
                dve.wait_ge(gate_step, 4)
                nc.vector.tensor_scalar(lg[:, 3, :], lg[:, 2, :], sc[:, 2:3], None, ALU.mult).then_inc(gate_step, 1)
                dve.wait_ge(gate_step, 5)
                p_j = lg[:, 3, :].unsqueeze(1).broadcast_to([8, E, E])
                p_e = lg[:, 3, :].unsqueeze(2).broadcast_to([8, E, E])
                nc.vector.tensor_tensor(cmp[:, :, 0, :], p_j, p_e, ALU.is_ge).then_inc(gate_step, 1)
                nc.vector.tensor_tensor(cmp[:, :, 1, :], p_j, p_e, ALU.is_gt).then_inc(gate_step, 1)
                dve.wait_ge(gate_step, 7)
                nc.vector.tensor_tensor(cmpm[:], cmp[:], order_mask, ALU.mult).then_inc(gate_step, 1)
                dve.wait_ge(gate_step, 8)
                nc.vector.tensor_reduce(lg[:, 4, :], cmpm[:].rearrange("p e t j -> p e (t j)"), AX.X,
                                        ALU.add).then_inc(gate_step, 1)
                dve.wait_ge(gate_step, 9)
                nc.vector.scalar_tensor_tensor(out=lg[:, 5, :], in0=lg[:, 4, :], scalar=1.5, in1=lg[:, 3, :],
                                               op0=ALU.is_lt, op1=ALU.mult,
                                               accum_out=sc[:, 3:4]).then_inc(gate_step, 1)
                dve.wait_ge(gate_step, 10)
                nc.vector.tensor_scalar(sc[:, 4:5], sc[:, 3:4], 1e-8, None, ALU.add).then_inc(gate_step, 1)
                dve.wait_ge(gate_step, 11)
                nc.vector.reciprocal(sc[:, 5:6], sc[:, 4:5]).then_inc(gate_step, 1)
                dve.wait_ge(gate_step, 12)
                nc.vector.tensor_scalar(lg[:, 6, :], lg[:, 5, :], sc[:, 5:6], None, ALU.mult).then_inc(gate_step, 1)
                dve.wait_ge(gate_step, 13)
                nc.vector.tensor_tensor(wdiag[:], lg[:, 6, :].unsqueeze(1).broadcast_to([8, B, E]),
                                        ident.unsqueeze(2).broadcast_to([8, B, E]), ALU.mult).then_inc(wdiag_ok, 1)

            def region_bias():
                def weight(e):
                    return wbc[:, :, e]

                def bias(e):
                    return cols[:, EB2 + e:EB2 + e + 1]

                dve.wait_ge(wbc_ok, 1)
                nc.vector.tensor_copy(wbc[:].rearrange("p b e -> p (b e)"), S[1][:, 0:B * E]).then_inc(wbc_copied, 1)
                dve.wait_ge(wbc_copied, 1)
                nc.vector.tensor_scalar(br[:, 3, :], weight(0), bias(0), bias(SHARED), ALU.mult,
                                        ALU.add).then_inc(br_step, 1)
                dve.wait_ge(br_step, 1)
                nc.vector.scalar_tensor_tensor(out=br[:, 4, :], in0=weight(3), scalar=bias(3), in1=br[:, 3, :],
                                               op0=ALU.mult, op1=ALU.add).then_inc(br_step, 1)
                dve.wait_ge(br_step, 2)
                nc.vector.scalar_tensor_tensor(out=br[:, 0, :], in0=weight(1), scalar=bias(1), in1=br[:, 4, :],
                                               op0=ALU.mult, op1=ALU.add).then_inc(br_step, 1)
                nc.vector.scalar_tensor_tensor(out=br[:, 2, :], in0=weight(2), scalar=bias(2), in1=br[:, 4, :],
                                               op0=ALU.mult, op1=ALU.add).then_inc(br_step, 1)
                dve.wait_ge(br_step, 4)
                nc.vector.scalar_tensor_tensor(out=br[:, 1, :], in0=weight(2), scalar=bias(2), in1=br[:, 0, :],
                                               op0=ALU.mult, op1=ALU.add).then_inc(br_step, 1)

            def x_plus_bias(hf):
                xs = half(hf)
                dve.wait_ge(br_step, 5)
                for g, (_, p0, n) in enumerate(REGIONS):
                    nc.vector.tensor_tensor(acc[:, xs, p0:p0 + n], xT[:, xs, p0:p0 + n],
                                            br[:, g, xs].unsqueeze(2).broadcast_to([128, HB, n]),
                                            ALU.add).then_inc(xb_ok, 1)

            def hidden_lo(i):
                _, e, _, _ = unit(i)
                lo, hi = SPAN[e]
                n = HB * (hi - lo)
                s = i % NH
                dve.wait_ge(hi_ok, i + 1)
                if i >= NH:
                    dve.wait_ge(y_ok, i - NH + 1)
                nc.vector.tensor_tensor(h_lo[:, s, 0:n], h[:, s, 0:n], h_hi[:, s, 0:n].bitcast(F32),
                                        ALU.subtract).then_inc(lo_ok, 1)

            def accumulate(u):
                hf, e = u // NE, ORDER[u % NE]
                lo, hi = SPAN[e]
                n = hi - lo
                dve.wait_ge(y_ok, NC * (u + 1))
                y = Y[u % 2]
                if e == SHARED:
                    dve.wait_ge(xb_ok, 3 * (hf + 1))
                    a = acc[:, half(hf), :].rearrange("p b t -> p (b t)")
                    nc.vector.tensor_tensor(a, y[:], a, ALU.add).then_inc(acc_ok, 1)
                    return
                dve.wait_ge(acc_ok, u)
                for j in range(HB):
                    b = hf * HB + j
                    ins = nc.vector.scalar_tensor_tensor(
                        out=acc[:, b, lo:hi], in0=y[:, j * n:(j + 1) * n], scalar=wbc[:, b, e:e + 1],
                        in1=acc[:, b, lo:hi], op0=ALU.mult, op1=ALU.add)
                    if u == HALVES * NE - 1 and b == PIECES[1][1] - 1:
                        ins.then_inc(acc_early, 1)
                ins.then_inc(acc_ok, 1)

            def widen():
                dve.wait_ge(hc_ok, 1)
                dve.wait_ge(consts_ok, 3)
                v = wide[:].rearrange("p (r k) -> p r k", k=STEP)

                def place(part):
                    return v[:, :, 64 * part:64 * part + 64].rearrange("p r (h s) -> p r h s", h=HALVES)[:, :, :, 0:HB]

                src = hc[:].rearrange("p (h j) -> p h j", h=HALVES).unsqueeze(1).broadcast_to([128, R, HALVES, HB])
                nc.vector.tensor_copy(place(0), src).then_inc(wide_ok, 1)
                dve.wait_ge(wide_ok, 1)
                nc.vector.tensor_tensor(place(1), src, place(0).bitcast(F32), ALU.subtract).then_inc(wide_ok, 1)

            def adaptive_biased():
                dve.wait_ge(adapt_ok, 1)
                dve.wait_ge(b2_in, 32)
                nc.vector.tensor_tensor(part[:], S[0][64:128, :], b2[:], ALU.add).then_inc(part_ok, 1)
                dve.wait_ge(part_ok, 1)
                nc.vector.tensor_tensor(lr[:].rearrange("p q d -> p (q d)"), S[0][0:64, :], part[:],
                                        ALU.add).then_inc(lr_ok, 1)

            def merge_out(m):
                hf, kind = m % 2, m // 2
                dst, fixed = ((WM, down), (WO, upT))[kind]
                dve.wait_ge(merge_ok, m + 1)
                nc.vector.tensor_tensor(dst[:, half(hf), :], S[1 + m % 2][:].rearrange("p (b n) -> p b n", b=HB),
                                        fixed.unsqueeze(1).broadcast_to([128, HB, 128]), ALU.add).then_inc(merged, 1)

            def result(n):
                b0, b1 = PIECES[n]
                dve.wait_ge(o_ok, n + 1)
                nc.vector.scalar_tensor_tensor(
                    out=oT[:, b0:b1, :].rearrange("p b t -> p (b t)"),
                    in0=acc[:, b0:b1, :].rearrange("p b t -> p (b t)"), scalar=2.0,
                    in1=OUT_BANK[n][:, 0:(b1 - b0) * T], op0=ALU.mult, op1=ALU.add).then_inc(o_copied, 1)

            layer_norm()
            x_lo_part(0)
            normed()
            weight_lo(0)
            affine_cond()
            silu()
            weight_hi(1)
            pool_tokens()
            weight_lo(1)
            gate_logits()
            weight_hi(2)
            gate_weights()
            weight_hi(3)
            side = {0: [lambda: weight_hi(4)], 1: [lambda: weight_hi(5)], 2: [widen], 4: [region_bias],
                    5: [lambda: x_plus_bias(0), lambda: weight_hi(6)], 6: [lambda: weight_hi(7)],
                    8: [lambda: x_lo_part(1)], 9: [lambda: weight_hi(8)], 10: [lambda: weight_hi(9)],
                    15: [lambda: x_plus_bias(1)], 23: [adaptive_biased]}
            for r in range(R):
                side.setdefault(11 + r, []).append(lambda r=r: adaptive_hi(r))
            for m in range(4):
                side.setdefault(26 + m, []).append(lambda m=m: merge_out(m))
            for i in range(CHUNKS + LAG):
                if i < CHUNKS:
                    hidden_lo(i)
                for job in side.get(i, []):
                    job()
                last = i - LAG
                if last >= 0 and last % NC == NC - 1:
                    accumulate(last // NC)
            for n in range(len(PIECES)):
                result(n)


def kernel(x, cond_1024, L0_cond_gate_w, L0_cond_gate_b, L0_cond_time_w, L0_cond_time_b, L0_cond_ew1, L0_cond_eb1,
           L0_cond_ew2, L0_cond_eb2, L0_cond_sw1, L0_cond_sb1, L0_cond_sw2, L0_cond_sb2, L1_cond_base_up,
           L1_cond_base_down, L1_cond_ln_gamma, L1_cond_ln_beta, L1_cond_W1, L1_cond_bias1, L1_cond_W2,
           L1_cond_bias2):
    import numpy as np
    import concourse.bacc as bacc
    from concourse import mybir as _mybir
    from concourse.bass_utils import run_bass_kernel_spmd

    x = np.asarray(x)
    B, T, D = x.shape
    E, _, H = L0_cond_ew1.shape
    Q = 4
    R = L1_cond_W2.shape[1] // (Q * D)
    f = x.dtype
    spans = [slice(t0, t0 + n) for t0, _, n in regions(T)]
    xT = np.transpose(x, (2, 0, 1))
    xT = np.concatenate([xT[:, :, s] for s in spans], axis=2)
    first = np.concatenate([L0_cond_ew1, np.asarray(L0_cond_sw1)[None]])
    second = np.concatenate([L0_cond_ew2, np.asarray(L0_cond_sw2)[None]])
    second = second.reshape(E + 1, H // 128, 128, D).transpose(0, 2, 1, 3).reshape(E + 1, 128, H * D // 128)
    w = np.concatenate([first, second], axis=2)
    eb1 = np.concatenate([L0_cond_eb1, np.asarray(L0_cond_sb1)[None]]).reshape(-1, 128).T
    eb2 = np.concatenate([L0_cond_eb2, np.asarray(L0_cond_sb2)[None]]).T
    three = np.stack([L1_cond_bias1, L1_cond_ln_gamma, L1_cond_ln_beta], axis=1)
    gw = np.asarray(L0_cond_gate_w).reshape(3, D, E).transpose(1, 0, 2).reshape(D, 3 * E)
    hb = B // 2
    own = np.zeros((128, hb), f)
    for p in range(2 * hb * R):
        own[p, p % hb] = 1
    cols = np.concatenate([np.asarray(cond_1024).T, eb1, eb2, three, gw, L0_cond_time_w, own], axis=1)
    order = np.zeros((8, E, 2, E), f)
    for e in range(E):
        order[:, e, 0, :e] = 1
        order[:, e, 1, e + 1:] = 1
    biases = np.zeros((8, 3 * E), f)
    biases[0, :E] = L0_cond_gate_b
    biases[0, E:] = L0_cond_time_b
    rows = np.concatenate([cond_1024, biases, np.eye(8, dtype=f), order.reshape(8, -1)], axis=1)
    base = np.stack([L1_cond_base_down, np.asarray(L1_cond_base_up).T, L1_cond_W1], axis=1)
    W2 = np.asarray(L1_cond_W2).reshape(128, Q * D, R).transpose(0, 2, 1)
    b2 = np.asarray(L1_cond_bias2).reshape(Q * D, R).T

    nc = bacc.Bacc("TRN2", target_bir_lowering=False, num_devices=1)
    arrays, args = {}, []
    for name, a in (("xT", xT), ("w", w), ("cols", cols), ("rows", rows), ("base", base), ("W2", W2), ("b2", b2)):
        arrays[f"in_{name}"] = np.ascontiguousarray(a)
        args.append(nc.dram_tensor(f"in_{name}", a.shape, _mybir.dt.from_np(a.dtype), kind="ExternalInput").ap())
    out = nc.dram_tensor("out_0", xT.shape, _mybir.dt.from_np(f), kind="ExternalOutput").ap()
    moe_lowrank_kernel(nc, *args, out)
    r = run_bass_kernel_spmd(nc, [arrays], core_ids=[0])
    oT = r.results[0]["out_0"]
    back = np.concatenate([oT[:, :, p0:p0 + n] for _, p0, n in sorted(regions(T))], axis=2)
    return np.ascontiguousarray(np.transpose(back, (1, 2, 0)))
```

```python
import math
from contextlib import ExitStack

import concourse.bass as bass
from concourse import mybir

ALU = mybir.AluOpType
ACT = mybir.ActivationFunctionType
AX = mybir.AxisListType
F32 = mybir.dt.float32
F32R = mybir.dt.float32r

EPS = 1e-5


def regions(T):
    third = T // 3
    rest = T - 2 * third
    return (0, 0, third), (2 * third, third, rest), (third, third + rest, third)


def moe_lowrank_kernel(nc, xT_d, w_d, cols_d, rows_d, base_d, W2_d, b2_d, out_d):
    D, B, T = xT_d.shape
    NE = w_d.shape[0]
    E = NE - 1
    SHARED = E
    NC = w_d.shape[2] // (2 * D)
    H = NC * 128
    R, QD = b2_d.shape
    Q = QD // D
    REGIONS = regions(T)
    HEAD, PROP = REGIONS[0][2], REGIONS[1][2]
    SPAN = {0: (0, T), 1: (0, HEAD + PROP), 2: (HEAD, T), 3: (0, T), SHARED: (0, T)}
    HALVES = 2
    HB = B // HALVES
    ORDER = (SHARED, 0, 3, 1, 2)
    CHUNKS = HALVES * NE * NC
    LAG = 3
    NZ, NH = 3, 5
    HALF_ROWS = HB * R
    STEP = 128 + HB

    def unit(i):
        u = i // NC
        return u // NE, ORDER[u % NE], i % NC, u

    with ExitStack() as ctx:
        def sb(name, shape, dt=F32):
            return ctx.enter_context(nc.sbuf_tensor(name, shape, dt))

        def pb(name):
            return ctx.enter_context(nc.psum_tensor(name, [128, 512], F32))

        def sem(name):
            return ctx.enter_context(nc.semaphore(name))

        xT = sb("xT", [128, B, T])
        w = sb("w", [128, NE, 2, H])
        cols = sb("cols", [128, cols_d.shape[1]])
        rows = sb("rows", [8, rows_d.shape[1]])
        base = sb("base", [128, 2, 128])
        W2 = sb("W2", [128, R, QD])
        b2 = sb("b2", [128, QD])
        EB1 = B
        EB2 = EB1 + NE * NC
        BIAS1 = EB2 + NE
        GAMMA, BETA = BIAS1 + 1, BIAS1 + 2
        GW = BETA + 1
        TW = GW + 3 * E
        OWN = TW + 2 * E
        condT = cols[:, 0:B]
        gw = cols[:, GW:TW].rearrange("p (k e) -> p k e", k=3)
        tw = cols[:, TW:OWN]
        own = cols[:, OWN:OWN + HB]
        is_lo = cols[:, OWN + HB:OWN + HB + 1]
        sign = cols[:, OWN + HB + 1:OWN + HB + 2]
        W1 = cols[:, OWN + HB + 2:OWN + HB + 130]
        cond = rows[:, 0:128]
        gate_b = rows[0:1, 128:128 + E]
        time_b = rows[0:1, 128 + E:128 + 3 * E]
        ident = rows[:, 128 + 3 * E:128 + 3 * E + 8]
        order_mask = rows[:, 136 + 3 * E:136 + 3 * E + 2 * E * E].rearrange("p (e t j) -> p e t j", e=E, t=2)
        down, upT = base[:, 0, :], base[:, 1, :]
        w_hi, w_lo = sb("w_hi", [128, NE, 2, H], F32R), sb("w_lo", [128, NE, 2, H], F32R)
        x_hi, x_lo = sb("x_hi", [128, B, T], F32R), sb("x_lo", [128, B, T], F32R)
        W2_hi, W2_lo = sb("W2_hi", [128, R, QD], F32R), sb("W2_lo", [128, R, QD], F32R)
        wide = sb("wide", [128, R * STEP], F32R)
        h = sb("h", [128, NH, 512])
        h_hi, h_lo = sb("h_hi", [128, NH, 512], F32R), sb("h_lo", [128, NH, 512], F32R)
        acc = sb("acc", [128, B, T])
        mid = sb("mid", [128, B, T])
        oT = sb("oT", [128, B, T])
        ones = sb("ones", [8, 128])
        table_probe = sb("table_probe", [1, 1])
        sums = sb("sums", [128, 3, B])
        joint = sb("joint", [128, 3, B])
        pooled = sb("pooled", [128, 3, B])
        sil = sb("sil", [128, 4, B])
        mod_s = sb("mod_s", [8, 2 * E])
        lg = sb("lg", [8, 7, E])
        sc = sb("sc", [8, 6])
        cmp = sb("cmp", [8, E, 2, E])
        cmpm = sb("cmpm", [8, E, 2, E])
        wdiag = sb("wdiag", [8, B, E])
        wbc = sb("wbc", [128, B, E])
        br = sb("br", [128, 5, B])
        powers = sb("powers", [128, 1 + B + E])
        stats = sb("stats", [8, 6])
        mv = sb("mv", [8, 4])
        cn = sb("cn", [8, 128])
        cT = sb("cT", [128, B])
        hc = sb("hc", [128, B])
        summand = sb("summand", [128, QD])
        other = sb("other", [128, QD])
        lr = sb("lr", [128, Q, D])
        lr_hi = sb("lr_hi", [128, Q, D], F32R)
        lr_lo = sb("lr_lo", [128, 2, D])
        kept = sb("kept", [128, 2, D])
        left = sb("left", [128, 2, D], F32R)
        spread = sb("spread", [128, 2, 2, HB, D], F32R)
        WM = sb("WM", [128, B, 128])
        WO = sb("WO", [128, B, 128])

        half_neg, inv_e, base_e = powers[0:8, 0:1], powers[:, 1:1 + B], powers[0:8, 1 + B:1 + B + E]

        Z = [pb(f"Z{i}") for i in range(NZ)]
        Y = [pb(f"Y{i}") for i in range(2)]
        S = [pb(f"S{i}") for i in range(3)]

        x_in = [sem(f"x_in{i}") for i in range(HALVES)]
        w_in = [sem(f"w_in{k}") for k in range(2 * NE)]
        cols_in = sem("cols_in")
        rows_in = sem("rows_in")
        base_in = sem("base_in")
        W2_in = [sem(f"W2_in{c}") for c in range(2)]
        b2_in = sem("b2_in")
        other_in = sem("other_in")
        out_done = sem("out_done")
        consts_ok = sem("consts_ok")
        b2_zero = sem("b2_zero")
        rstd_ok = sem("rstd_ok")
        exp_sil = sem("exp_sil")
        exp_ok = sem("exp_ok")
        x1_lo = sem("x1_lo")
        xb_ok = sem("xb_ok")
        w_lo_pool = sem("w_lo_pool")
        W2_lo_ok = sem("W2_lo_ok")
        spread_ok = sem("spread_ok")
        cnT_ok = sem("cnT_ok")
        hpre_ok = sem("hpre_ok")
        logit_ok = sem("logit_ok")
        wbc_ok = sem("wbc_ok")
        adapt_ok = sem("adapt_ok")
        merge_ok = sem("merge_ok")
        z_ok = sem("z_ok")
        y_ok = sem("y_ok")
        mid_ok = sem("mid_ok")
        o_ok = sem("o_ok")
        probed = sem("probed")
        x0_hi = sem("x0_hi")
        hc_ok = sem("hc_ok")
        h_ok = sem("h_ok")
        hi_ok = sem("hi_ok")
        last_hi = sem("last_hi")
        midg_ok = sem("midg_ok")
        ln_step = sem("ln_step")
        cn_ok = sem("cn_ok")
        cT_ok = sem("cT_ok")
        x1_hi = sem("x1_hi")
        x_lo_ok = sem("x_lo_ok")
        w_hi_ok = sem("w_hi_ok")
        w_hi_act = sem("w_hi_act")
        w_lo_ok = sem("w_lo_ok")
        W2_hi_ok = sem("W2_hi_ok")
        pool_step = sem("pool_step")
        sil_step = sem("sil_step")
        gate_step = sem("gate_step")
        nmax_ok = sem("nmax_ok")
        shifted_ok = sem("shifted_ok")
        logits_read = sem("logits_read")
        wdiag_ok = sem("wdiag_ok")
        wbc_copied = sem("wbc_copied")
        br_step = sem("br_step")
        wide_ok = sem("wide_ok")
        summand_ok = sem("summand_ok")
        lr_ok = sem("lr_ok")
        lr_hi_ok = sem("lr_hi_ok")
        lr_lo_ok = sem("lr_lo_ok")
        kept_ok = sem("kept_ok")
        left_ok = sem("left_ok")
        merged = sem("merged")
        lo_ok = sem("lo_ok")
        acc_ok = sem("acc_ok")
        acc_early = sem("acc_early")
        o_copied = sem("o_copied")

        ACT_HI = (0, 5, 7, 9)
        DVE_LO = 1

        def w_part(tile, k):
            return tile[:, ORDER[k // 2], k % 2, :]

        def wait_hi(eng, k):
            if k in ACT_HI:
                eng.wait_ge(w_hi_act, ACT_HI.index(k) + 1)
            else:
                eng.wait_ge(w_hi_ok, k - sum(j < k for j in ACT_HI) + 1)

        def wait_split(eng, k):
            if k < DVE_LO:
                eng.wait_ge(w_lo_ok, k + 1)
            else:
                eng.wait_ge(w_lo_pool, k - DVE_LO + 1)

        def half(hf):
            return slice(hf * HB, (hf + 1) * HB)

        PIECES = ((0, HB), (HB, HB + HB // 2), (HB + HB // 2, B))
        MID_BANK = (S[0], S[1], Z[0])
        OUT_BANK = (S[2], Z[1], Z[2])

        block = ctx.enter_context(nc.Block())

        @block.sync
        def _(sp):
            def load_w(k):
                e, f = ORDER[k // 2], k % 2
                sp.dma_start(w[:, e, f, :], w_d[e, :, f * H:(f + 1) * H]).then_inc(w_in[k], 16)

            sp.dma_start(rows[:], rows_d).then_inc(rows_in, 16)
            sp.dma_start(xT[:, half(0), :], xT_d[:, half(0), :]).then_inc(x_in[0], 16)
            sp.dma_start(cols[:], cols_d).then_inc(cols_in, 16)
            load_w(0)
            load_w(1)
            sp.dma_start(xT[:, half(1), :], xT_d[:, half(1), :]).then_inc(x_in[1], 16)
            for k in range(2, 2 * NE):
                load_w(k)
            for c in range(2):
                rs = slice(c * R // 2, (c + 1) * R // 2)
                sp.dma_start(W2[:, rs, :], W2_d[:, rs, :]).then_inc(W2_in[c], 16)
            sp.dma_start(base[:], base_d).then_inc(base_in, 16)
            sp.wait_ge(b2_zero, 1)
            for hf in range(HALVES):
                sp.dma_start(b2[hf * 64:hf * 64 + HALF_ROWS, :],
                             b2_d.unsqueeze(1).broadcast_to([R, HB, QD])).then_inc(b2_in, 16)
            sp.wait_ge(summand_ok, 1)
            for p0 in range(0, 128, 32):
                p1 = p0 + 32 if p0 % 64 == 0 else p0 - 32
                sp.dma_start(other[p0:p0 + 32, :], summand[p1:p1 + 32, :]).then_inc(other_in, 16)
            for n, (b0, b1) in enumerate(PIECES):
                sp.wait_ge(o_copied, n + 1)
                sp.dma_start(out_d[:, b0:b1, :], oT[:, b0:b1, :]).then_inc(out_done, 16)
            sp.wait_ge(out_done, 16 * len(PIECES))

        @block.gpsimd
        def _(pool):
            pool.memset(wide[:].bitcast(F32), 0.0).then_inc(consts_ok, 1)
            pool.memset(half_neg, -0.5).then_inc(consts_ok, 1)
            pool.memset(inv_e, math.exp(-1)).then_inc(consts_ok, 1)
            pool.memset(base_e, math.e).then_inc(consts_ok, 1)
            pool.memset(ones[:], 1.0).then_inc(consts_ok, 1)
            pool.memset(b2[:], 0.0).then_inc(b2_zero, 1)
            pool.wait_ge(ln_step, 3)
            pool.wait_ge(consts_ok, 4)
            pool.tensor_tensor(mv[:, 3:4], mv[:, 2:3], half_neg, ALU.pow).then_inc(rstd_ok, 1)
            pool.wait_ge(cols_in, 16)
            pool.tensor_tensor(sil[:, 0, :], inv_e, condT, ALU.pow).then_inc(exp_sil, 1)
            def weight_lo(k):
                wait_hi(pool, k)
                pool.tensor_tensor(w_part(w_lo, k), w_part(w, k), w_part(w_hi, k).bitcast(F32),
                                   ALU.subtract).then_inc(w_lo_pool, 1)

            def add_bias(hf, src):
                xs = half(hf)
                for g, (_, p0, n) in enumerate(REGIONS):
                    pool.tensor_tensor(acc[:, xs, p0:p0 + n], src[:, xs, p0:p0 + n],
                                       br[:, g, xs].unsqueeze(2).broadcast_to([128, HB, n]),
                                       ALU.add).then_inc(xb_ok, 1)

            for k in range(DVE_LO, 5):
                weight_lo(k)
            pool.wait_ge(shifted_ok, 1)
            pool.tensor_tensor(lg[:, 2, :], base_e, lg[:, 0, :], ALU.pow).then_inc(exp_ok, 1)
            for k in range(5, 2 * NE):
                weight_lo(k)
            pool.wait_ge(x1_hi, 1)
            pool.tensor_tensor(x_lo[:, half(1), :], xT[:, half(1), :], x_hi[:, half(1), :].bitcast(F32),
                               ALU.subtract).then_inc(x1_lo, 1)
            for r in range(R):
                pool.wait_ge(W2_hi_ok, r + 1)
                pool.tensor_tensor(W2_lo[:, r, :], W2[:, r, :], W2_hi[:, r, :].bitcast(F32),
                                   ALU.subtract).then_inc(W2_lo_ok, 1)
            pool.wait_ge(br_step, 5)
            add_bias(1, xT)
            pool.wait_ge(lr_hi_ok, 1)
            for kind, q in ((0, 3), (1, 0)):
                for part in range(2):
                    src = lr_hi[:, q, :].bitcast(F32)
                    if part == 1:
                        pool.wait_ge(lr_lo_ok, 1)
                        src = lr_lo[:, q // 3, :]
                    pool.tensor_tensor(spread[:, kind, part], src.unsqueeze(1).broadcast_to([128, HB, D]),
                                       own.unsqueeze(2).broadcast_to([128, HB, D]),
                                       ALU.mult).then_inc(spread_ok, 1)
            pool.wait_ge(acc_ok, NE)
            add_bias(0, acc)

        @block.scalar
        def _(act):
            def weight_hi(k):
                act.wait_ge(w_in[k], 16)
                nc.scalar.activation(w_part(w_hi, k), w_part(w, k), ACT.Copy).then_inc(w_hi_act, 1)

            act.wait_ge(consts_ok, 5)
            nc.scalar.activation(table_probe[:], ones[0:1, 0:1], ACT.Gelu).then_inc(probed, 1)
            act.wait_ge(x_in[0], 16)
            nc.scalar.activation(x_hi[:, half(0), :], xT[:, half(0), :], ACT.Copy).then_inc(x0_hi, 1)
            weight_hi(0)
            act.wait_ge(cols_in, 16)
            act.wait_ge(hpre_ok, 1)
            nc.scalar.activation(hc[:], S[2][:, 0:B], ACT.Gelu, bias=cols[:, BIAS1:BIAS1 + 1]).then_inc(hc_ok, 1)

            def gelu(i):
                _, e, c, _ = unit(i)
                lo, hi = SPAN[e]
                n = HB * (hi - lo)
                act.wait_ge(z_ok, i + 1)
                if i >= NH:
                    act.wait_ge(lo_ok, i - NH + 1)
                b = EB1 + e * NC + c
                nc.scalar.activation(h[:, i % NH, 0:n], Z[i % NZ][:, 0:n], ACT.Gelu_apprx_tanh,
                                     bias=cols[:, b:b + 1]).then_inc(h_ok, 1)

            def hidden_hi(i):
                _, e, _, _ = unit(i)
                lo, hi = SPAN[e]
                n = HB * (hi - lo)
                act.wait_ge(h_ok, i + 1)
                if i >= NH:
                    act.wait_ge(y_ok, i - NH + 1)
                nc.scalar.activation(h_hi[:, i % NH, 0:n], h[:, i % NH, 0:n], ACT.Copy).then_inc(hi_ok, 1)

            weight_at = {3: 5, 6: 7, 8: 9}
            gelu(0)
            hidden_hi(0)
            gelu(1)
            for i in range(2, CHUNKS - 1):
                gelu(i)
                hidden_hi(i - 1)
                if i in weight_at:
                    weight_hi(weight_at[i])
            hidden_hi(CHUNKS - 2)
            gelu(CHUNKS - 1)
            for n, (b0, b1) in enumerate(PIECES):
                act.wait_ge(mid_ok, n + 1)
                nc.scalar.activation(mid[:, b0:b1, :].rearrange("p b t -> p (b t)"),
                                     MID_BANK[n][:, 0:(b1 - b0) * T], ACT.Gelu).then_inc(midg_ok, 1)

        @block.tensor
        def _(pe):
            def warm_up(products):
                pe.wait_ge(consts_ok, 1)
                for _ in range(products):
                    pe.matmul(Y[0][:], wide[:, 0:128], wide[:, 0:512], start=True, stop=True)

            def cond_turned():
                pe.wait_ge(rows_in, 16)
                pe.wait_ge(cn_ok, 1)
                pe.transpose(S[1][:, 0:B], cn[:], ident).then_inc(cnT_ok, 1)

            def cond_hidden():
                pe.wait_ge(cols_in, 16)
                pe.wait_ge(cT_ok, 1)
                pe.matmul(S[2][:, 0:B], W1, cT[:], start=True, stop=True).then_inc(hpre_ok, 1)

            def z_product(i):
                hf, e, c, _ = unit(i)
                lo, hi = SPAN[e]
                n = hi - lo
                if c == 0 and i > 0:
                    wait_split(pe, 2 * ORDER.index(e))
                    pe.wait_ge((x_lo_ok, x1_lo)[hf], 1)
                if i >= NZ:
                    pe.wait_ge(h_ok, i - NZ + 1)
                o = Z[i % NZ][:, 0:HB * n].rearrange("p (b t) -> p b t", b=HB)
                xs = half(hf)
                ws = slice(c * 128, (c + 1) * 128)
                if i == 0:
                    pe.wait_ge(x0_hi, 1)
                    wait_hi(pe, 0)
                pe.matmul(o, w_hi[:, e, 0, ws], x_hi[:, xs, lo:hi], start=True, stop=False)
                if i == 0:
                    pe.wait_ge(x_lo_ok, 1)
                pe.matmul(o, w_hi[:, e, 0, ws], x_lo[:, xs, lo:hi], start=False, stop=False)
                if i == 0:
                    wait_split(pe, 0)
                pe.matmul(o, w_lo[:, e, 0, ws], x_hi[:, xs, lo:hi], start=False, stop=True).then_inc(z_ok, 1)

            def y_product(i):
                _, e, c, u = unit(i)
                lo, hi = SPAN[e]
                n = HB * (hi - lo)
                if c == 0:
                    wait_split(pe, 2 * ORDER.index(e) + 1)
                    if u >= 2:
                        pe.wait_ge(acc_ok, u - 1)
                if i < CHUNKS - 1:
                    pe.wait_ge(hi_ok, i + 1)
                else:
                    pe.wait_ge(last_hi, 1)
                o = Y[u % 2][:, 0:n]
                s = i % NH
                ws = slice(c * 128, (c + 1) * 128)
                pe.matmul(o, w_hi[:, e, 1, ws], h_hi[:, s, 0:n], start=(c == 0), stop=False)
                pe.matmul(o, w_lo[:, e, 1, ws], h_hi[:, s, 0:n], start=False, stop=False)
                pe.wait_ge(lo_ok, i + 1)
                pe.matmul(o, w_hi[:, e, 1, ws], h_lo[:, s, 0:n], start=False, stop=(c == NC - 1)).then_inc(y_ok, 1)

            def logits():
                pe.wait_ge(consts_ok, 5)
                pe.wait_ge(sil_step, 3)
                pe.matmul(S[0][0:8, 8:8 + 2 * E], sil[:, 3, :], tw, start=True, stop=False)
                pe.matmul(S[0][0:8, 8:8 + 2 * E], ones[0:1, 0:8], time_b, start=False, stop=True)
                pe.wait_ge(pool_step, 7)
                for k in range(3):
                    pe.matmul(S[0][0:8, 0:E], pooled[:, k, :], gw[:, k, :], start=(k == 0), stop=False)
                pe.matmul(S[0][0:8, 0:E], ones[0:1, 0:8], gate_b, start=False, stop=True).then_inc(logit_ok, 1)

            def spread_weights():
                pe.wait_ge(wdiag_ok, 1)
                pe.matmul(S[1][:, 0:B * E], ones[:], wdiag[:].rearrange("p b e -> p (b e)"),
                          start=True, stop=True).then_inc(wbc_ok, 1)

            def adaptive(r0, r1):
                pe.wait_ge(wide_ok, 2)
                pe.wait_ge(logits_read, 1)
                for r in range(r0, r1):
                    pe.wait_ge(W2_lo_ok, r + 1)
                    ws = wide[:, r * 128:(r + 1) * 128]
                    pe.matmul(S[0][:], ws, W2_hi[:, r, :], start=(r == 0), stop=False)
                    mm = pe.matmul(S[0][:], ws, W2_lo[:, r, :], start=False, stop=(r == R - 1))
                if r1 == R:
                    mm.then_inc(adapt_ok, 1)

            def merge(m):
                hf, kind = m % 2, m // 2
                rr = slice(hf * 64, hf * 64 + 2 * HALF_ROWS)
                r0 = slice(hf * 64, hf * 64 + HALF_ROWS)
                pe.wait_ge(left_ok, 1)
                pe.wait_ge(spread_ok, 2 * (kind + 1))
                if m == 0:
                    pe.wait_ge(wbc_copied, 1)
                elif m == 1:
                    pe.wait_ge(hc_ok, 1)
                else:
                    pe.wait_ge(merged, m - 1)
                hi, lo = (spread[:, kind, part].rearrange("p b n -> p (b n)") for part in range(2))
                pe.matmul(S[1 + m % 2][:], left[rr, 1 - kind, :], hi[rr], start=True, stop=False)
                pe.matmul(S[1 + m % 2][:], left[r0, 1 - kind, :], lo[r0], start=False, stop=True).then_inc(merge_ok, 1)

            def mid_product(n):
                b0, b1 = PIECES[n]
                if n == 0:
                    pe.wait_ge(xb_ok, 6)
                    pe.wait_ge(summand_ok, 1)
                    pe.wait_ge(merged, 2)
                elif n == 1:
                    pe.wait_ge(acc_early, 1)
                    pe.wait_ge(merged, 3)
                else:
                    pe.wait_ge(acc_ok, HALVES * NE)
                for b in range(b0, b1):
                    j = b - b0
                    mm = pe.matmul(MID_BANK[n][:, j * T:(j + 1) * T], WM[:, b, :], acc[:, b, :], start=True, stop=True)
                mm.then_inc(mid_ok, 1)

            def out_product(n):
                b0, b1 = PIECES[n]
                pe.wait_ge(midg_ok, n + 1)
                pe.wait_ge(merged, 4)
                for b in range(b0, b1):
                    j = b - b0
                    mm = pe.matmul(OUT_BANK[n][:, j * T:(j + 1) * T], WO[:, b, :], mid[:, b, :], start=True, stop=True)
                mm.then_inc(o_ok, 1)

            side = {5: [logits], 11: [spread_weights],
                    33: [lambda: merge(0)], 34: [lambda: merge(1)], 37: [lambda: merge(2)], 38: [lambda: merge(3)],
                    CHUNKS + 1: [lambda: mid_product(0)]}
            for r in range(R):
                side[15 + r] = [lambda r=r: adaptive(r, r + 1)]
            warm_up(6)
            cond_turned()
            warm_up(2)
            cond_hidden()
            for i in range(CHUNKS + LAG):
                if i < CHUNKS:
                    z_product(i)
                for job in side.get(i, []):
                    job()
                if i >= LAG:
                    y_product(i - LAG)
            out_product(0)
            mid_product(1)
            mid_product(2)
            out_product(1)
            out_product(2)


        @block.vector
        def _(dve):
            def weight_hi(k):
                dve.wait_ge(w_in[k], 16)
                nc.vector.tensor_copy(w_part(w_hi, k), w_part(w, k)).then_inc(w_hi_ok, 1)

            def weight_lo(k):
                wait_hi(dve, k)
                nc.vector.tensor_tensor(w_part(w_lo, k), w_part(w, k), w_part(w_hi, k).bitcast(F32),
                                        ALU.subtract).then_inc(w_lo_ok, 1)

            def x_lo_part(hf):
                xs = half(hf)
                dve.wait_ge(x0_hi, 1)
                nc.vector.tensor_tensor(x_lo[:, xs, :], xT[:, xs, :], x_hi[:, xs, :].bitcast(F32),
                                        ALU.subtract).then_inc(x_lo_ok, 1)

            def x1_hi_part():
                dve.wait_ge(x_in[1], 16)
                nc.vector.tensor_copy(x_hi[:, half(1), :], xT[:, half(1), :]).then_inc(x1_hi, 1)

            def adaptive_hi(r):
                dve.wait_ge(W2_in[r // (R // 2)], 16)
                nc.vector.tensor_copy(W2_hi[:, r, :], W2[:, r, :]).then_inc(W2_hi_ok, 1)

            def layer_norm():
                dve.wait_ge(rows_in, 16)
                nc.vector.bn_stats(stats[:], cond).then_inc(ln_step, 1)
                dve.wait_ge(ln_step, 1)
                nc.vector.bn_aggr(mv[:, 0:2], stats[:]).then_inc(ln_step, 1)
                dve.wait_ge(ln_step, 2)
                nc.vector.tensor_scalar(mv[:, 2:3], mv[:, 1:2], EPS, None, ALU.add).then_inc(ln_step, 1)

            def normed():
                dve.wait_ge(rstd_ok, 1)
                nc.vector.tensor_scalar(cn[:], cond, mv[:, 0:1], mv[:, 3:4], ALU.subtract, ALU.mult).then_inc(cn_ok, 1)

            def affine_cond():
                dve.wait_ge(cols_in, 16)
                dve.wait_ge(cnT_ok, 1)
                nc.vector.tensor_scalar(cT[:], S[1][:, 0:B], cols[:, GAMMA:GAMMA + 1], cols[:, BETA:BETA + 1],
                                        ALU.mult, ALU.add).then_inc(cT_ok, 1)

            def silu_sum():
                dve.wait_ge(exp_sil, 1)
                nc.vector.tensor_scalar(sil[:, 1, :], sil[:, 0, :], 1.0, None, ALU.add).then_inc(sil_step, 1)

            def silu():
                dve.wait_ge(sil_step, 1)
                nc.vector.reciprocal(sil[:, 2, :], sil[:, 1, :]).then_inc(sil_step, 1)
                dve.wait_ge(sil_step, 2)
                nc.vector.tensor_tensor(sil[:, 3, :], sil[:, 2, :], condT, ALU.mult).then_inc(sil_step, 1)

            def sum_tokens():
                dve.wait_ge(x_in[0], 16)
                dve.wait_ge(x_in[1], 16)
                for g, (_, p0, n) in enumerate(REGIONS):
                    nc.vector.tensor_reduce(sums[:, g, :], xT[:, :, p0:p0 + n], AX.X, ALU.add).then_inc(pool_step, 1)

            def pool_tokens():
                dve.wait_ge(pool_step, 3)
                nc.vector.tensor_tensor(joint[:, 1:3, :], sums[:, 0:3:2, :],
                                        sums[:, 1, :].unsqueeze(1).broadcast_to([128, 2, B]),
                                        ALU.add).then_inc(pool_step, 1)

            def pool_all():
                dve.wait_ge(pool_step, 4)
                nc.vector.tensor_tensor(joint[:, 0, :], joint[:, 1, :], sums[:, 2, :], ALU.add).then_inc(pool_step, 1)
                nc.vector.tensor_scalar(pooled[:, 1:3, :], joint[:, 1:3, :], 1.0 / (HEAD + PROP), None,
                                        ALU.mult).then_inc(pool_step, 1)

            def pool_mean():
                dve.wait_ge(pool_step, 6)
                nc.vector.tensor_scalar(pooled[:, 0, :], joint[:, 0, :], 1.0 / T, None, ALU.mult).then_inc(pool_step, 1)

            def gate_scaled():
                dve.wait_ge(logit_ok, 1)
                nc.vector.tensor_copy(mod_s[:], S[0][0:8, 8:8 + 2 * E]).then_inc(gate_step, 1)
                dve.wait_ge(gate_step, 1)
                nc.vector.scalar_tensor_tensor(out=lg[:, 0, :], in0=mod_s[:, 0:E], scalar=1.0, in1=S[0][0:8, 0:E],
                                               op0=ALU.add, op1=ALU.mult).then_inc(logits_read, 1)

            def gate_shifted():
                dve.wait_ge(logits_read, 1)
                nc.vector.tensor_tensor(lg[:, 1, :], lg[:, 0, :], mod_s[:, E:2 * E], ALU.add).then_inc(gate_step, 1)

            def gate_max():
                dve.wait_ge(gate_step, 2)
                nc.vector.tensor_reduce(sc[:, 0:1], lg[:, 1, :], AX.X, ALU.max, negate=True).then_inc(nmax_ok, 1)
                dve.wait_ge(nmax_ok, 1)
                nc.vector.tensor_scalar(lg[:, 0, :], lg[:, 1, :], sc[:, 0:1], None, ALU.add).then_inc(shifted_ok, 1)

            def gate_exp_sum():
                dve.wait_ge(exp_ok, 1)
                nc.vector.tensor_reduce(sc[:, 1:2], lg[:, 2, :], AX.X, ALU.add).then_inc(gate_step, 1)

            def gate_softmax():
                dve.wait_ge(gate_step, 3)
                nc.vector.reciprocal(sc[:, 2:3], sc[:, 1:2]).then_inc(gate_step, 1)
                dve.wait_ge(gate_step, 4)
                nc.vector.tensor_scalar(lg[:, 3, :], lg[:, 2, :], sc[:, 2:3], None, ALU.mult).then_inc(gate_step, 1)

            def gate_compare():
                dve.wait_ge(gate_step, 5)
                p_j = lg[:, 3, :].unsqueeze(1).broadcast_to([8, E, E])
                p_e = lg[:, 3, :].unsqueeze(2).broadcast_to([8, E, E])
                nc.vector.tensor_tensor(cmp[:, :, 0, :], p_j, p_e, ALU.is_ge).then_inc(gate_step, 1)
                nc.vector.tensor_tensor(cmp[:, :, 1, :], p_j, p_e, ALU.is_gt).then_inc(gate_step, 1)

            def gate_order():
                dve.wait_ge(gate_step, 7)
                nc.vector.tensor_tensor(cmpm[:], cmp[:], order_mask, ALU.mult).then_inc(gate_step, 1)

            def gate_rank():
                dve.wait_ge(gate_step, 8)
                nc.vector.tensor_reduce(lg[:, 4, :], cmpm[:].rearrange("p e t j -> p e (t j)"), AX.X,
                                        ALU.add).then_inc(gate_step, 1)

            def gate_largest():
                dve.wait_ge(gate_step, 9)
                nc.vector.scalar_tensor_tensor(out=lg[:, 5, :], in0=lg[:, 4, :], scalar=1.5, in1=lg[:, 3, :],
                                               op0=ALU.is_lt, op1=ALU.mult,
                                               accum_out=sc[:, 3:4]).then_inc(gate_step, 1)

            def gate_norm():
                dve.wait_ge(gate_step, 10)
                nc.vector.tensor_scalar(sc[:, 4:5], sc[:, 3:4], 1e-8, None, ALU.add).then_inc(gate_step, 1)

            def gate_inverse():
                dve.wait_ge(gate_step, 11)
                nc.vector.reciprocal(sc[:, 5:6], sc[:, 4:5]).then_inc(gate_step, 1)

            def gate_weights():
                dve.wait_ge(gate_step, 12)
                nc.vector.tensor_scalar(lg[:, 6, :], lg[:, 5, :], sc[:, 5:6], None, ALU.mult).then_inc(gate_step, 1)

            def gate_blocks():
                dve.wait_ge(gate_step, 13)
                nc.vector.tensor_tensor(wdiag[:], lg[:, 6, :].unsqueeze(1).broadcast_to([8, B, E]),
                                        ident.unsqueeze(2).broadcast_to([8, B, E]), ALU.mult).then_inc(wdiag_ok, 1)

            def copy_weights():
                dve.wait_ge(wbc_ok, 1)
                nc.vector.tensor_copy(wbc[:].rearrange("p b e -> p (b e)"), S[1][:, 0:B * E]).then_inc(wbc_copied, 1)

            def region_bias():
                def weight(e):
                    return wbc[:, :, e]

                def bias(e):
                    return cols[:, EB2 + e:EB2 + e + 1]

                dve.wait_ge(wbc_copied, 1)
                nc.vector.tensor_scalar(br[:, 3, :], weight(0), bias(0), bias(SHARED), ALU.mult,
                                        ALU.add).then_inc(br_step, 1)
                dve.wait_ge(br_step, 1)
                nc.vector.scalar_tensor_tensor(out=br[:, 4, :], in0=weight(3), scalar=bias(3), in1=br[:, 3, :],
                                               op0=ALU.mult, op1=ALU.add).then_inc(br_step, 1)
                dve.wait_ge(br_step, 2)
                nc.vector.scalar_tensor_tensor(out=br[:, 0, :], in0=weight(1), scalar=bias(1), in1=br[:, 4, :],
                                               op0=ALU.mult, op1=ALU.add).then_inc(br_step, 1)
                nc.vector.scalar_tensor_tensor(out=br[:, 2, :], in0=weight(2), scalar=bias(2), in1=br[:, 4, :],
                                               op0=ALU.mult, op1=ALU.add).then_inc(br_step, 1)
                dve.wait_ge(br_step, 4)
                nc.vector.scalar_tensor_tensor(out=br[:, 1, :], in0=weight(2), scalar=bias(2), in1=br[:, 0, :],
                                               op0=ALU.mult, op1=ALU.add).then_inc(br_step, 1)

            def hidden_lo(i):
                _, e, _, _ = unit(i)
                lo, hi = SPAN[e]
                n = HB * (hi - lo)
                s = i % NH
                if i == CHUNKS - 1:
                    dve.wait_ge(h_ok, i + 1)
                    nc.vector.tensor_copy(h_hi[:, s, 0:n], h[:, s, 0:n]).then_inc(last_hi, 1)
                    dve.wait_ge(last_hi, 1)
                else:
                    dve.wait_ge(hi_ok, i + 1)
                if i >= NH:
                    dve.wait_ge(y_ok, i - NH + 1)
                nc.vector.tensor_tensor(h_lo[:, s, 0:n], h[:, s, 0:n], h_hi[:, s, 0:n].bitcast(F32),
                                        ALU.subtract).then_inc(lo_ok, 1)

            def accumulate(u, batches=range(HB)):
                hf, e = u // NE, ORDER[u % NE]
                lo, hi = SPAN[e]
                n = hi - lo
                dve.wait_ge(y_ok, NC * (u + 1))
                y = Y[u % 2]
                if e == SHARED:
                    src = xT
                    if hf == 1:
                        dve.wait_ge(xb_ok, 3)
                        src = acc
                    nc.vector.tensor_tensor(acc[:, half(hf), :].rearrange("p b t -> p (b t)"), y[:],
                                            src[:, half(hf), :].rearrange("p b t -> p (b t)"),
                                            ALU.add).then_inc(acc_ok, 1)
                    return
                dve.wait_ge(acc_ok, u)
                dve.wait_ge(wbc_copied, 1)
                for j in batches:
                    b = hf * HB + j
                    ins = nc.vector.scalar_tensor_tensor(
                        out=acc[:, b, lo:hi], in0=y[:, j * n:(j + 1) * n], scalar=wbc[:, b, e:e + 1],
                        in1=acc[:, b, lo:hi], op0=ALU.mult, op1=ALU.add)
                    if u == HALVES * NE - 1 and b == PIECES[1][1] - 1:
                        ins.then_inc(acc_early, 1)
                if j == HB - 1:
                    ins.then_inc(acc_ok, 1)

            def widen():
                dve.wait_ge(hc_ok, 1)
                dve.wait_ge(consts_ok, 1)
                v = wide[:].rearrange("p (r k) -> p r k", k=STEP)

                def place(part):
                    return v[:, :, 0:128].rearrange("p r (h q s) -> p r h q s", h=HALVES, q=2)[:, :, :, part, 0:HB]

                src = hc[:].rearrange("p (h j) -> p h j", h=HALVES).unsqueeze(1).broadcast_to([128, R, HALVES, HB])
                nc.vector.tensor_copy(place(0), src).then_inc(wide_ok, 1)
                dve.wait_ge(wide_ok, 1)
                nc.vector.tensor_tensor(place(1), src, place(0).bitcast(F32), ALU.subtract).then_inc(wide_ok, 1)

            def adaptive_out():
                dve.wait_ge(adapt_ok, 1)
                dve.wait_ge(b2_in, 32)
                dve.wait_ge(b2_zero, 1)
                nc.vector.tensor_tensor(summand[:], S[0][:], b2[:], ALU.add).then_inc(summand_ok, 1)

            def adaptive_sum():
                dve.wait_ge(other_in, 64)
                nc.vector.tensor_tensor(lr[:].rearrange("p q d -> p (q d)"), summand[:], other[:],
                                        ALU.add).then_inc(lr_ok, 1)

            def adaptive_split():
                dve.wait_ge(lr_ok, 1)
                nc.vector.tensor_copy(lr_hi[:], lr[:]).then_inc(lr_hi_ok, 1)
                dve.wait_ge(lr_hi_ok, 1)
                nc.vector.tensor_tensor(lr_lo[:], lr[:, 0:4:3, :], lr_hi[:, 0:4:3, :].bitcast(F32),
                                        ALU.subtract).then_inc(lr_lo_ok, 1)

            def adaptive_left():
                nc.vector.tensor_scalar(kept[:], lr[:, 1:3, :], is_lo, None, ALU.mult).then_inc(kept_ok, 1)
                dve.wait_ge(lr_hi_ok, 1)
                dve.wait_ge(kept_ok, 1)
                nc.vector.scalar_tensor_tensor(out=left[:], in0=lr_hi[:, 1:3, :].bitcast(F32), scalar=sign,
                                               in1=kept[:], op0=ALU.mult, op1=ALU.add).then_inc(left_ok, 1)

            def merge_out(m):
                hf, kind = m % 2, m // 2
                dst, fixed = ((WM, down), (WO, upT))[kind]
                dve.wait_ge(base_in, 16)
                dve.wait_ge(merge_ok, m + 1)
                nc.vector.tensor_tensor(dst[:, half(hf), :], S[1 + m % 2][:].rearrange("p (b n) -> p b n", b=HB),
                                        fixed.unsqueeze(1).broadcast_to([128, HB, 128]), ALU.add).then_inc(merged, 1)

            def result(n):
                b0, b1 = PIECES[n]
                dve.wait_ge(o_ok, n + 1)
                nc.vector.scalar_tensor_tensor(
                    out=oT[:, b0:b1, :].rearrange("p b t -> p (b t)"),
                    in0=acc[:, b0:b1, :].rearrange("p b t -> p (b t)"), scalar=2.0,
                    in1=OUT_BANK[n][:, 0:(b1 - b0) * T], op0=ALU.mult, op1=ALU.add).then_inc(o_copied, 1)

            layer_norm()
            normed()
            affine_cond()
            x_lo_part(0)
            weight_lo(0)
            weight_hi(1)
            sum_tokens()
            weight_hi(2)
            side = {0: [silu_sum, lambda: weight_hi(3), silu, pool_tokens, pool_all],
                    1: [pool_mean, lambda: weight_hi(4)],
                    2: [gate_scaled, lambda: weight_hi(6), gate_shifted], 3: [gate_max, lambda: weight_hi(8)],
                    4: [gate_exp_sum, gate_softmax], 5: [gate_compare, gate_order, gate_rank],
                    6: [gate_largest, lambda: accumulate(0), gate_norm],
                    7: [gate_inverse, x1_hi_part, gate_weights, widen, gate_blocks], 10: [copy_weights],
                    20: [region_bias], 22: [adaptive_out], 27: [adaptive_sum], 28: [adaptive_split],
                    29: [adaptive_left],
                    32: [lambda: merge_out(0)], 33: [lambda: merge_out(1)],
                    36: [lambda: merge_out(2)], 37: [lambda: merge_out(3)]}
            for r, i in enumerate((9, 11, 12, 13, 14, 16, 16, 17)):
                side.setdefault(i, []).append(lambda r=r: adaptive_hi(r))
            for u in range(1, HALVES * NE - 1):
                i = NC * (u + 1) - 1 + LAG
                if u % NE == 0:
                    side.setdefault(i, []).append(lambda u=u: accumulate(u))
                elif u == HALVES * NE - 2:
                    side.setdefault(i + 1, []).append(lambda u=u: accumulate(u))
                else:
                    side.setdefault(i, []).append(lambda u=u: accumulate(u, range(HB // 2)))
                    side.setdefault(i + 1, []).insert(0, lambda u=u: accumulate(u, range(HB // 2, HB)))
            for i in range(CHUNKS):
                hidden_lo(i)
                for job in side.get(i, []):
                    job()
            accumulate(HALVES * NE - 1)
            for n in range(len(PIECES)):
                result(n)


def kernel(x, cond_1024, L0_cond_gate_w, L0_cond_gate_b, L0_cond_time_w, L0_cond_time_b, L0_cond_ew1, L0_cond_eb1,
           L0_cond_ew2, L0_cond_eb2, L0_cond_sw1, L0_cond_sb1, L0_cond_sw2, L0_cond_sb2, L1_cond_base_up,
           L1_cond_base_down, L1_cond_ln_gamma, L1_cond_ln_beta, L1_cond_W1, L1_cond_bias1, L1_cond_W2,
           L1_cond_bias2):
    import numpy as np
    import concourse.bacc as bacc
    from concourse import mybir as _mybir
    from concourse.bass_utils import run_bass_kernel_spmd

    x = np.asarray(x)
    B, T, D = x.shape
    E, _, H = L0_cond_ew1.shape
    Q = 4
    R = L1_cond_W2.shape[1] // (Q * D)
    f = x.dtype
    spans = [slice(t0, t0 + n) for t0, _, n in regions(T)]
    xT = np.transpose(x, (2, 0, 1))
    xT = np.concatenate([xT[:, :, s] for s in spans], axis=2)
    first = np.concatenate([L0_cond_ew1, np.asarray(L0_cond_sw1)[None]])
    second = np.concatenate([L0_cond_ew2, np.asarray(L0_cond_sw2)[None]])
    second = second.reshape(E + 1, H // 128, 128, D).transpose(0, 2, 1, 3).reshape(E + 1, 128, H * D // 128)
    w = np.concatenate([first, second], axis=2)
    eb1 = np.concatenate([L0_cond_eb1, np.asarray(L0_cond_sb1)[None]]).reshape(-1, 128).T
    eb2 = np.concatenate([L0_cond_eb2, np.asarray(L0_cond_sb2)[None]]).T
    three = np.stack([L1_cond_bias1, L1_cond_ln_gamma, L1_cond_ln_beta], axis=1)
    gw = np.asarray(L0_cond_gate_w).reshape(3, D, E).transpose(1, 0, 2).reshape(D, 3 * E)
    hb = B // 2
    own = np.zeros((128, hb), f)
    part = np.zeros((128, 2), f)
    for p in range(128):
        own[p, p % hb] = 1
        part[p] = (1, -1) if p // 32 % 2 else (0, 1)
    cols = np.concatenate([np.asarray(cond_1024).T, eb1, eb2, three, gw, L0_cond_time_w, own, part, L1_cond_W1], axis=1)
    order = np.zeros((8, E, 2, E), f)
    for e in range(E):
        order[:, e, 0, :e] = 1
        order[:, e, 1, e + 1:] = 1
    biases = np.zeros((8, 3 * E), f)
    biases[0, :E] = L0_cond_gate_b
    biases[0, E:] = L0_cond_time_b
    rows = np.concatenate([cond_1024, biases, np.eye(8, dtype=f), order.reshape(8, -1)], axis=1)
    base = np.stack([L1_cond_base_down, np.asarray(L1_cond_base_up).T], axis=1)
    W2 = np.asarray(L1_cond_W2).reshape(128, Q * D, R).transpose(0, 2, 1)
    b2 = np.asarray(L1_cond_bias2).reshape(Q * D, R).T

    nc = bacc.Bacc("TRN2", target_bir_lowering=False, num_devices=1)
    arrays, args = {}, []
    for name, a in (("xT", xT), ("w", w), ("cols", cols), ("rows", rows), ("base", base), ("W2", W2), ("b2", b2)):
        arrays[f"in_{name}"] = np.ascontiguousarray(a)
        args.append(nc.dram_tensor(f"in_{name}", a.shape, _mybir.dt.from_np(a.dtype), kind="ExternalInput").ap())
    out = nc.dram_tensor("out_0", xT.shape, _mybir.dt.from_np(f), kind="ExternalOutput").ap()
    moe_lowrank_kernel(nc, *args, out)
    r = run_bass_kernel_spmd(nc, [arrays], core_ids=[0])
    oT = r.results[0]["out_0"]
    back = np.concatenate([oT[:, :, p0:p0 + n] for _, p0, n in sorted(regions(T))], axis=2)
    return np.ascontiguousarray(np.transpose(back, (1, 2, 0)))
```
